# Optimizing a Trainium2 kernel written in Bass

```python
import numpy as np
import jax
import jax.numpy as jnp

def _softmax(x, axis=-1):
    return jax.nn.softmax(x, axis=axis)

def _gelu(x):
    return jax.nn.gelu(x, approximate=True)

def _silu(x):
    return jax.nn.silu(x)

def _sigmoid(x):
    return jax.nn.sigmoid(x)

def _layernorm(x, axis=-1, eps=1e-05):
    m = jnp.mean(x, axis=axis, keepdims=True)
    v = jnp.var(x, axis=axis, keepdims=True)
    return (x - m) / jnp.sqrt(v + eps)

def _scatter_add(tgt, idx, src, axis=0):
    return tgt.at[idx].add(src)

def _segment_sum(src, seg, n):
    return jax.ops.segment_sum(src, seg, n)
kernel_name = 'mk_dlrm_tower_d1_rec_r8_6a60c3'

def setup_inputs(seed: int=0):
    np.random.seed(seed)
    _w = jnp.asarray

    def _rec_inputs():
        import jax
        import jax.numpy as jnp
        _tk = jax.random.key(seed)
        dense_ctx = jax.random.normal(jax.random.fold_in(_tk, 190), (512, 16), jnp.float32)
        ids = jnp.stack([jax.random.randint(jax.random.fold_in(_tk, 200 + f), (512,), 0, v, jnp.int32) for f, v in enumerate([125000, 1000, 1000, 1250, 1250, 1000, 125000, 125000, 1250, 1250, 12500, 1000, 12500, 125000, 1250, 1250, 1000, 1250, 125000, 1000, 1000, 1000, 12500, 1250, 1250, 1250, 125000, 1250, 1000, 125000, 125000, 12500, 12500, 1250, 125000, 1250, 1000, 1000, 12500])], axis=1)
        tbl_0 = 0.05 * jax.random.normal(jax.random.fold_in(_tk, 500 + 0), (125000, 16), jnp.float32)
        tbl_1 = 0.05 * jax.random.normal(jax.random.fold_in(_tk, 500 + 1), (1000, 16), jnp.float32)
        tbl_2 = 0.05 * jax.random.normal(jax.random.fold_in(_tk, 500 + 2), (1000, 16), jnp.float32)
        tbl_3 = 0.05 * jax.random.normal(jax.random.fold_in(_tk, 500 + 3), (1250, 16), jnp.float32)
        tbl_4 = 0.05 * jax.random.normal(jax.random.fold_in(_tk, 500 + 4), (1250, 16), jnp.float32)
        tbl_5 = 0.05 * jax.random.normal(jax.random.fold_in(_tk, 500 + 5), (1000, 16), jnp.float32)
        tbl_6 = 0.05 * jax.random.normal(jax.random.fold_in(_tk, 500 + 6), (125000, 16), jnp.float32)
        tbl_7 = 0.05 * jax.random.normal(jax.random.fold_in(_tk, 500 + 7), (125000, 16), jnp.float32)
        tbl_8 = 0.05 * jax.random.normal(jax.random.fold_in(_tk, 500 + 8), (1250, 16), jnp.float32)
        tbl_9 = 0.05 * jax.random.normal(jax.random.fold_in(_tk, 500 + 9), (1250, 16), jnp.float32)
        tbl_10 = 0.05 * jax.random.normal(jax.random.fold_in(_tk, 500 + 10), (12500, 16), jnp.float32)
        tbl_11 = 0.05 * jax.random.normal(jax.random.fold_in(_tk, 500 + 11), (1000, 16), jnp.float32)
        tbl_12 = 0.05 * jax.random.normal(jax.random.fold_in(_tk, 500 + 12), (12500, 16), jnp.float32)
        tbl_13 = 0.05 * jax.random.normal(jax.random.fold_in(_tk, 500 + 13), (125000, 16), jnp.float32)
        tbl_14 = 0.05 * jax.random.normal(jax.random.fold_in(_tk, 500 + 14), (1250, 16), jnp.float32)
        tbl_15 = 0.05 * jax.random.normal(jax.random.fold_in(_tk, 500 + 15), (1250, 16), jnp.float32)
        tbl_16 = 0.05 * jax.random.normal(jax.random.fold_in(_tk, 500 + 16), (1000, 16), jnp.float32)
        tbl_17 = 0.05 * jax.random.normal(jax.random.fold_in(_tk, 500 + 17), (1250, 16), jnp.float32)
        tbl_18 = 0.05 * jax.random.normal(jax.random.fold_in(_tk, 500 + 18), (125000, 16), jnp.float32)
        tbl_19 = 0.05 * jax.random.normal(jax.random.fold_in(_tk, 500 + 19), (1000, 16), jnp.float32)
        tbl_20 = 0.05 * jax.random.normal(jax.random.fold_in(_tk, 500 + 20), (1000, 16), jnp.float32)
        tbl_21 = 0.05 * jax.random.normal(jax.random.fold_in(_tk, 500 + 21), (1000, 16), jnp.float32)
        tbl_22 = 0.05 * jax.random.normal(jax.random.fold_in(_tk, 500 + 22), (12500, 16), jnp.float32)
        tbl_23 = 0.05 * jax.random.normal(jax.random.fold_in(_tk, 500 + 23), (1250, 16), jnp.float32)
        tbl_24 = 0.05 * jax.random.normal(jax.random.fold_in(_tk, 500 + 24), (1250, 16), jnp.float32)
        tbl_25 = 0.05 * jax.random.normal(jax.random.fold_in(_tk, 500 + 25), (1250, 16), jnp.float32)
        tbl_26 = 0.05 * jax.random.normal(jax.random.fold_in(_tk, 500 + 26), (125000, 16), jnp.float32)
        tbl_27 = 0.05 * jax.random.normal(jax.random.fold_in(_tk, 500 + 27), (1250, 16), jnp.float32)
        tbl_28 = 0.05 * jax.random.normal(jax.random.fold_in(_tk, 500 + 28), (1000, 16), jnp.float32)
        tbl_29 = 0.05 * jax.random.normal(jax.random.fold_in(_tk, 500 + 29), (125000, 16), jnp.float32)
        tbl_30 = 0.05 * jax.random.normal(jax.random.fold_in(_tk, 500 + 30), (125000, 16), jnp.float32)
        tbl_31 = 0.05 * jax.random.normal(jax.random.fold_in(_tk, 500 + 31), (12500, 16), jnp.float32)
        tbl_32 = 0.05 * jax.random.normal(jax.random.fold_in(_tk, 500 + 32), (12500, 16), jnp.float32)
        tbl_33 = 0.05 * jax.random.normal(jax.random.fold_in(_tk, 500 + 33), (1250, 16), jnp.float32)
        tbl_34 = 0.05 * jax.random.normal(jax.random.fold_in(_tk, 500 + 34), (125000, 16), jnp.float32)
        tbl_35 = 0.05 * jax.random.normal(jax.random.fold_in(_tk, 500 + 35), (1250, 16), jnp.float32)
        tbl_36 = 0.05 * jax.random.normal(jax.random.fold_in(_tk, 500 + 36), (1000, 16), jnp.float32)
        tbl_37 = 0.05 * jax.random.normal(jax.random.fold_in(_tk, 500 + 37), (1000, 16), jnp.float32)
        tbl_38 = 0.05 * jax.random.normal(jax.random.fold_in(_tk, 500 + 38), (12500, 16), jnp.float32)
        _rk = jax.random.fold_in(_tk, 7)
        W_top1 = 0.05 * jax.random.normal(jax.random.fold_in(_tk, 801), (400, 512), jnp.float32)
        W_top2 = 0.0441942 * jax.random.normal(jax.random.fold_in(_tk, 802), (512, 256), jnp.float32)
        W_top3 = 0.0625 * jax.random.normal(jax.random.fold_in(_tk, 803), (256, 1), jnp.float32)
        b_top1 = jnp.zeros((512,), jnp.float32)
        b_top2 = jnp.zeros((256,), jnp.float32)
        return (dense_ctx, ids, tbl_0, tbl_1, tbl_2, tbl_3, tbl_4, tbl_5, tbl_6, tbl_7, tbl_8, tbl_9, tbl_10, tbl_11, tbl_12, tbl_13, tbl_14, tbl_15, tbl_16, tbl_17, tbl_18, tbl_19, tbl_20, tbl_21, tbl_22, tbl_23, tbl_24, tbl_25, tbl_26, tbl_27, tbl_28, tbl_29, tbl_30, tbl_31, tbl_32, tbl_33, tbl_34, tbl_35, tbl_36, tbl_37, tbl_38, W_top1, b_top1, W_top2, b_top2, W_top3)
    dense_ctx, ids, tbl_0, tbl_1, tbl_2, tbl_3, tbl_4, tbl_5, tbl_6, tbl_7, tbl_8, tbl_9, tbl_10, tbl_11, tbl_12, tbl_13, tbl_14, tbl_15, tbl_16, tbl_17, tbl_18, tbl_19, tbl_20, tbl_21, tbl_22, tbl_23, tbl_24, tbl_25, tbl_26, tbl_27, tbl_28, tbl_29, tbl_30, tbl_31, tbl_32, tbl_33, tbl_34, tbl_35, tbl_36, tbl_37, tbl_38, W_top1, b_top1, W_top2, b_top2, W_top3 = _rec_inputs()

    def _L0_rec_setup():
        import jax, jax.numpy as jnp
        import numpy as np
        B, F0, D = (256, 39, 16)
        CROSS = [128, 128, 128]
        key = jax.random.key(seed)
        k0, k1, k2, k3 = jax.random.split(key, 4)
        inputs = jax.random.normal(k0, (B, F0, D), dtype=jnp.float32)
        f0 = jax.random.normal(k1, (F0 * F0, CROSS[0]), dtype=jnp.float32) * 0.05
        f1 = jax.random.normal(k2, (CROSS[0] * F0, CROSS[1]), dtype=jnp.float32) * 0.05
        f2 = jax.random.normal(k3, (CROSS[1] * F0, CROSS[2]), dtype=jnp.float32) * 0.05
        return {'inputs': inputs, 'f0': f0, 'f1': f1, 'f2': f2}
    _L0_rec_all = _L0_rec_setup()
    _L0_rec_in = {k: v for k, v in _L0_rec_all.items() if k in ('f0', 'f1', 'f2')}
    del _L0_rec_all
    return {'dense_ctx': dense_ctx, 'ids': ids, 'tbl_0': tbl_0, 'tbl_1': tbl_1, 'tbl_2': tbl_2, 'tbl_3': tbl_3, 'tbl_4': tbl_4, 'tbl_5': tbl_5, 'tbl_6': tbl_6, 'tbl_7': tbl_7, 'tbl_8': tbl_8, 'tbl_9': tbl_9, 'tbl_10': tbl_10, 'tbl_11': tbl_11, 'tbl_12': tbl_12, 'tbl_13': tbl_13, 'tbl_14': tbl_14, 'tbl_15': tbl_15, 'tbl_16': tbl_16, 'tbl_17': tbl_17, 'tbl_18': tbl_18, 'tbl_19': tbl_19, 'tbl_20': tbl_20, 'tbl_21': tbl_21, 'tbl_22': tbl_22, 'tbl_23': tbl_23, 'tbl_24': tbl_24, 'tbl_25': tbl_25, 'tbl_26': tbl_26, 'tbl_27': tbl_27, 'tbl_28': tbl_28, 'tbl_29': tbl_29, 'tbl_30': tbl_30, 'tbl_31': tbl_31, 'tbl_32': tbl_32, 'tbl_33': tbl_33, 'tbl_34': tbl_34, 'tbl_35': tbl_35, 'tbl_36': tbl_36, 'tbl_37': tbl_37, 'tbl_38': tbl_38, 'W_top1': W_top1, 'b_top1': b_top1, 'W_top2': W_top2, 'b_top2': b_top2, 'W_top3': W_top3, 'L0_rec_f0': _L0_rec_in['f0'], 'L0_rec_f1': _L0_rec_in['f1'], 'L0_rec_f2': _L0_rec_in['f2']}

def reference(dense_ctx, ids, tbl_0, tbl_1, tbl_2, tbl_3, tbl_4, tbl_5, tbl_6, tbl_7, tbl_8, tbl_9, tbl_10, tbl_11, tbl_12, tbl_13, tbl_14, tbl_15, tbl_16, tbl_17, tbl_18, tbl_19, tbl_20, tbl_21, tbl_22, tbl_23, tbl_24, tbl_25, tbl_26, tbl_27, tbl_28, tbl_29, tbl_30, tbl_31, tbl_32, tbl_33, tbl_34, tbl_35, tbl_36, tbl_37, tbl_38, W_top1, b_top1, W_top2, b_top2, W_top3, L0_rec_f0, L0_rec_f1, L0_rec_f2):
    import jax
    import jax.numpy as jnp

    def _L0_rec_ref(inputs, f0, f1, f2):
        import jax, jax.numpy as jnp
        import numpy as np
        B, F0, D = (256, 39, 16)
        CROSS = [128, 128, 128]
        filters = [f0, f1, f2]
        x0 = inputs
        xk = inputs
        outs = []
        for W in filters:
            b, f, d = x0.shape
            g = xk.shape[1]
            z = jnp.einsum('bfd,bgd->bfgd', x0, xk).reshape(b, f * g, d)
            cur = jnp.einsum('bpd,pm->bmd', z, W)
            outs.append(cur)
            xk = cur
        result = jnp.concatenate(outs, axis=1)
        return jnp.sum(result, axis=-1)
    e = jnp.stack([tbl_0[ids[:, 0]], tbl_1[ids[:, 1]], tbl_2[ids[:, 2]], tbl_3[ids[:, 3]], tbl_4[ids[:, 4]], tbl_5[ids[:, 5]], tbl_6[ids[:, 6]], tbl_7[ids[:, 7]], tbl_8[ids[:, 8]], tbl_9[ids[:, 9]], tbl_10[ids[:, 10]], tbl_11[ids[:, 11]], tbl_12[ids[:, 12]], tbl_13[ids[:, 13]], tbl_14[ids[:, 14]], tbl_15[ids[:, 15]], tbl_16[ids[:, 16]], tbl_17[ids[:, 17]], tbl_18[ids[:, 18]], tbl_19[ids[:, 19]], tbl_20[ids[:, 20]], tbl_21[ids[:, 21]], tbl_22[ids[:, 22]], tbl_23[ids[:, 23]], tbl_24[ids[:, 24]], tbl_25[ids[:, 25]], tbl_26[ids[:, 26]], tbl_27[ids[:, 27]], tbl_28[ids[:, 28]], tbl_29[ids[:, 29]], tbl_30[ids[:, 30]], tbl_31[ids[:, 31]], tbl_32[ids[:, 32]], tbl_33[ids[:, 33]], tbl_34[ids[:, 34]], tbl_35[ids[:, 35]], tbl_36[ids[:, 36]], tbl_37[ids[:, 37]], tbl_38[ids[:, 38]]], axis=1)
    z = _L0_rec_ref(e, L0_rec_f0, L0_rec_f1, L0_rec_f2)
    z = z.reshape(z.shape[0], -1)
    h = jnp.concatenate([z, dense_ctx], axis=1)
    h = jnp.maximum(h @ W_top1 + b_top1, 0.0)
    h = jnp.maximum(h @ W_top2 + b_top2, 0.0)
    y = h @ W_top3
    return y

_drawn_inputs = setup_inputs


def setup_inputs(seed=0):
    import zlib

    import numpy as np

    out = dict(_drawn_inputs(seed))
    spreads = {'b_top1': (0.0, 0.618), 'b_top2': (0.0, 0.286)}
    factors = {'tbl_0': 4.315,
     'tbl_1': 5.198,
     'tbl_2': 4.715,
     'tbl_3': 5.107,
     'tbl_4': 5.116,
     'tbl_5': 5.123,
     'tbl_6': 4.77,
     'tbl_7': 4.773,
     'tbl_8': 5.136,
     'tbl_9': 5.057,
     'tbl_10': 5.022,
     'tbl_11': 4.628,
     'tbl_12': 4.25,
     'tbl_13': 4.373,
     'tbl_14': 4.592,
     'tbl_15': 5.068,
     'tbl_16': 4.984,
     'tbl_17': 4.893,
     'tbl_18': 5.478,
     'tbl_19': 5.236,
     'tbl_20': 4.897,
     'tbl_21': 4.843,
     'tbl_22': 4.512,
     'tbl_23': 4.774,
     'tbl_24': 4.508,
     'tbl_25': 4.474,
     'tbl_26': 4.882,
     'tbl_27': 4.801,
     'tbl_28': 5.079,
     'tbl_29': 4.887,
     'tbl_30': 4.784,
     'tbl_31': 4.505,
     'tbl_32': 5.082,
     'tbl_33': 4.618,
     'tbl_34': 4.792,
     'tbl_35': 4.498,
     'tbl_36': 4.919,
     'tbl_37': 5.211,
     'tbl_38': 4.744,
     'L0_rec_f1': 5.031,
     'L0_rec_f2': 8.0}
    for name, (base, spread) in spreads.items():
        noise = np.random.default_rng([zlib.crc32(name.encode()), seed]).standard_normal(out[name].shape)
        drawn = base * np.exp(spread * noise) if base else spread * noise
        out[name] = jnp.asarray(drawn.astype(out[name].dtype))
    for name, factor in factors.items():
        out[name] = (out[name] * factor).astype(out[name].dtype)
    return out
```

```python
import numpy as np
import concourse.bass as bass
from concourse import mybir
from contextlib import ExitStack

B, F, D, M = 512, 39, 16, 128
P = 128
BLOCKS = B // P
TB = P // D
CHUNKS = 4
TILES = 4
CPOS = TILES * P
CB = TILES * TB
LO = 64
KX = LO + F
SH = 3
NT = 7
NSHIFT = (F + 1) // 2
PR = SH * F
FG = 4
NG = 10
ZF = TB * F
ZC = ZF + TB
PAD = 2 * TB
H1, H2 = 512, 256
DC = 16


def fields(g):
    return range(FG * g, min(FG * (g + 1), F))


ACT_GROUPS = [g for g in range(NG) if g % 2 == 0]
DVE_GROUPS = [g for g in range(NG) if g % 2 == 1]
NA, ND = len(ACT_GROUPS), len(DVE_GROUPS)
DVE_FIELDS = sum(len(fields(g)) for g in DVE_GROUPS)
FOLDS = NA

SLOTS = TILES * NG
T_SLOT = {2: 0, 4: 1, 6: 2, 8: 3}
X0T_SLOT = 12
REP_SLOT = 13
ROLL_SLOT = {14 + 2 * t: t for t in range(NT)}
L0_SLOT = {19 + 2 * t: t for t in range(NT)}
X1_SLOT = 33


def program(nc, ids, tables, w0a, w0b, w1, w2, wt1, bt1, wt2, bt2, wt3, ctx_t, sel_d, selt_d, ident_d, mask_d, out):
    f32 = mybir.dt.float32
    f32r = mybir.dt.float32r
    i32 = mybir.dt.int32
    ALU = mybir.AluOpType
    ACT = mybir.ActivationFunctionType
    AX = mybir.AxisListType

    stack = ExitStack()
    with stack:
        def sb(name, shape, dt=f32):
            return stack.enter_context(nc.sbuf_tensor(name, shape, dt))

        def pb(name):
            return stack.enter_context(nc.psum_tensor(name, [P, 512], f32))

        def sem(name):
            return stack.enter_context(nc.semaphore(name))

        w1h = sb("w1h", [P, F, M], f32r)
        w1l = sb("w1l", [P, F, M], f32r)
        w2s = sb("w2s", [P, F, M])
        z_all = sb("z_all", [P, F, PAD + B])
        w1raw = z_all[:, :, :].rearrange("p f b -> p (f b)")[:, 0:F * M]
        w0braw = z_all[0:PR, :, :].rearrange("p f b -> p (f b)")[:, F * M:F * M + NT * M]
        selraw = z_all[0:KX, :, :].rearrange("p f b -> p (f b)")[:, 7000:7000 + (NT + 1) * PR]
        seltraw = z_all[0:KX, :, :].rearrange("p f b -> p (f b)")[:, 8000:8000 + F + 1]
        w0s = sb("w0s", [PR, NT, M])
        x1h = sb("x1h", [P, 2, CPOS], f32r)
        x1l = sb("x1l", [P, 2, CPOS], f32r)
        xs = sb("xs", [P, P, D], f32r)
        sel = sb("sel", [KX, NT + 1, PR], f32r)
        selt = sb("selt", [KX, F + 1], f32r)
        ident = sb("ident", [P, P])
        mask = sb("mask", [P, TB])
        bdiag = sb("bdiag", [P, TILES, ZC])
        x0t = sb("x0t", [P, 2, TILES, F + 1])
        cur1 = sb("cur1", [P, TILES, M])
        acc = sb("acc", [P, 2, 2, M])
        fold = sb("fold", [P, 2, FG * M])
        out0 = sb("out0", [P, B])
        out1 = sb("out1", [P, PAD + B])
        idx = sb("idx", [P, F], i32)
        b1c = sb("b1c", [P, H1 // P])
        b2c = sb("b2c", [P, H2 // P])
        w3c = sb("w3c", [P, H2 // P])
        ctx_sb = sb("ctx_sb", [DC, B])
        yrow = sb("yrow", [1, B])
        arena = sb("arena", [P, 22528 // 4])
        prod = arena[:, 0:2560].rearrange("p (s f m) -> p s f m", s=5, f=FG)
        rep = arena[0:PR, 2560:3072]
        z = arena[0:PR, 3072:4608].rearrange("p (s n) -> p s n", s=3)
        emb = arena[:, 4608:4608 + F * D].rearrange("p (f d) -> p f d", d=D)
        wt1_sb = arena[:, 0:2048].rearrange("p (k n) -> p k n", k=4)
        wt2_sb = arena[:, 2048:3072].rearrange("p (k n) -> p k n", k=4)
        h1 = arena[:, 3072:5120].rearrange("p (k n) -> p k n", k=4)
        out2 = arena[:, 5120:5632]
        h2 = fold

        ya = [pb("ya0"), pb("ya1")]
        yd = [pb("yd0"), pb("yd1")]
        roll = [pb("roll0"), pb("roll1")]
        c0 = pb("c0")
        misc = pb("misc")

        idx_in = sem("idx_in")
        const_in = sem("const_in")
        w1_in = sem("w1_in")
        late_in = sem("late_in")
        mlp_in = sem("mlp_in")
        emb_in = sem("emb_in")
        out_done = sem("out_done")
        pads_zero = sem("pads_zero")
        startup = sem("startup")
        sel_ready = sem("sel_ready")
        w0_ready = sem("w0_ready")
        w1h_ready = sem("w1h_ready")
        w1l_ready = sem("w1l_ready")
        emb_used = sem("emb_used")
        t_start = sem("t_start")
        misc_full = sem("misc_full")
        misc_free = sem("misc_free")
        xs_hi = sem("xs_hi")
        xs_ready = sem("xs_ready")
        x0t_ready = sem("x0t_ready")
        rep_full = sem("rep_full")
        rep_ready = sem("rep_ready")
        roll_full = sem("roll_full")
        z_ready = sem("z_ready")
        l0_done = sem("l0_done")
        x1_hi = sem("x1_hi")
        x1_ready = sem("x1_ready")
        ya_full = sem("ya_full")
        yd_full = sem("yd_full")
        prod_ready = sem("prod_ready")
        acc_step = sem("acc_step")
        fold_step = sem("fold_step")
        bdiag_ready = sem("bdiag_ready")
        half_step = sem("half_step")
        cur1_ready = sem("cur1_ready")
        z_in = sem("z_in")
        o2_full = sem("o2_full")
        o2_ready = sem("o2_ready")
        h1_full = sem("h1_full")
        h1_ready = sem("h1_ready")
        h2_full = sem("h2_full")
        h2_ready = sem("h2_ready")
        y_full = sem("y_full")
        y_ready = sem("y_ready")

        block = stack.enter_context(nc.Block())

        def misc_base(bt, k):
            return bt * (5 * CHUNKS + 4) + 5 + 5 * k

        def misc_use(bt, k, what, n=0):
            extra = 4 if k == CHUNKS - 1 else 0
            at = {"t": 1 + n, "x0t": 2 + extra, "z": (0, 1 + extra, 3 + extra, 4 + extra)[n]}[what]
            return misc_base(bt, k) + at

        def z_use(bt, k, q, last):
            if last and k == CHUNKS - 1:
                return misc_base(bt, k) + q
            return misc_use(bt, k, "z", q)

        FLUSH = 5 + (BLOCKS - 1) * (5 * CHUNKS + 4) + 5 * (CHUNKS - 1) + TILES

        @block.sync
        def _(sp):
            sp.dma_start(idx[:], ids[0:P, :]).then_inc(idx_in, 16)
            sp.dma_start(selraw, sel_d).then_inc(const_in, 16)
            sp.dma_start(seltraw, selt_d).then_inc(const_in, 16)
            sp.dma_start(ident[:], ident_d).then_inc(const_in, 16)
            sp.dma_start(mask[:], mask_d).then_inc(const_in, 16)
            sp.dma_start(w0s[:].rearrange("p t m -> p (t m)"), w0a).then_inc(const_in, 16)
            sp.dma_start(w0braw, w0b).then_inc(const_in, 16)
            sp.dma_start(w1raw.rearrange("p (f m) -> p f m", m=M), w1.rearrange("(f g) m -> g f m", g=M)).then_inc(w1_in, 16)
            sp.dma_start(w2s[:], w2.rearrange("(f g) m -> g f m", g=M)).then_inc(late_in, 16)
            sp.dma_start(b1c[:], bt1).then_inc(late_in, 16)
            sp.dma_start(b2c[:], bt2).then_inc(late_in, 16)
            sp.dma_start(w3c[:], wt3).then_inc(late_in, 16)
            sp.dma_start(ctx_sb[:], ctx_t).then_inc(late_in, 16)
            with sp.Fori(0, BLOCKS - 1) as bt:
                sp.wait_ge(emb_in, bt * (16 * F) + 16 * F)
                sp.dma_start(idx[:], ids[bass.ds(bt * P + P, P), :]).then_inc(idx_in, 16)
            sp.wait_ge(cur1_ready, BLOCKS * 16 + 2)
            sp.wait_ge(x1_ready, BLOCKS * CHUNKS)
            sp.dma_start(wt1_sb[:, 0:3, :], wt1[0:3 * P, :].rearrange("(k p) n -> p k n", p=P)).then_inc(mlp_in, 16)
            sp.dma_start(wt1_sb[0:DC, 3, :], wt1[3 * P:3 * P + DC, :]).then_inc(mlp_in, 16)
            sp.dma_start(wt2_sb, wt2.rearrange("(k p) n -> p k n", p=P)).then_inc(mlp_in, 16)
            sp.wait_ge(y_ready, 1)
            sp.dma_start(out.rearrange("b o -> o b"), yrow[:]).then_inc(out_done, 16)
            sp.wait_ge(out_done, 16)

        @block.gpsimd
        def _(pool):
            def gather(f):
                nc.gpsimd.indirect_dma_start(emb[:, f, :], None, tables[f],
                                             bass.IndirectOffsetOnAxis(ap=idx[:, f:f + 1], axis=0)).then_inc(emb_in, 16)

            nc.gpsimd.memset(xs[32:LO, :, :].bitcast(f32), 0.0).then_inc(pads_zero, 1)
            pool.wait_ge(idx_in, 16)
            for f in range(F):
                gather(f)

            def tile_sum(tau, q, extra):
                s = q % 2
                total = fold[:, s, :]
                base = (tau + 1) * FOLDS

                def group(j):
                    return prod[:, j, :, :].rearrange("p f m -> p (f m)")
                pool.wait_ge(prod_ready, tau * NA + 4)
                pool.wait_ge(cur1_ready, tau + 1)
                nc.gpsimd.tensor_tensor(total, group(0), group(1), ALU.add).then_inc(fold_step, 1)
                extra()
                for j in range(2, NA):
                    pool.wait_ge(prod_ready, tau * NA + j + 3)
                    pool.wait_ge(fold_step, base + j - 1)
                    nc.gpsimd.tensor_tensor(total, total, group(j), ALU.add).then_inc(fold_step, 1)
                    extra()
                pool.wait_ge(fold_step, base + NA - 1)
                nc.gpsimd.tensor_tensor(fold[:, s, 0:2 * M], fold[:, s, 0:2 * M], fold[:, s, 2 * M:4 * M],
                                        ALU.add).then_inc(fold_step, 1)

            def block_body(bt, last):
                queue = [] if last else list(range(F))
                every = 0

                def extra():
                    if queue:
                        gather(queue.pop(0))
                if not last:
                    pool.wait_ge(idx_in, bt * 16 + 32)
                    pool.wait_ge(emb_used, bt + 1)
                for t in range(CHUNKS * TILES):
                    tile_sum(bt * 16 + t, t % TILES, extra)

            with pool.Fori(0, BLOCKS - 1) as bt:
                block_body(bt, False)
            block_body(BLOCKS - 1, True)

        @block.scalar
        def _(act):
            act.sem_inc(misc_free, 1)
            act.sem_inc(prod_ready, 2)
            act.wait_ge(const_in, 16 * 6)
            nc.scalar.activation(sel[:].rearrange("p t r -> p (t r)"), selraw, ACT.Copy).then_inc(sel_ready, 1)
            nc.scalar.activation(selt[:], seltraw, ACT.Copy).then_inc(sel_ready, 1)
            act.wait_ge(w1_in, 16)
            nc.scalar.activation(w1h[:].rearrange("p f m -> p (f m)"), w1raw, ACT.Copy).then_inc(w1h_ready, 1)

            def t_hi(n, use, j):
                act.wait_ge(misc_full, use + 1)
                act.wait_ge(pads_zero, 1)
                nc.scalar.activation(xs[0:F, :, 4 * j:4 * j + 4], misc[0:F, :].rearrange("p (d b) -> p b d", d=4), ACT.Copy)\
                    .then_inc(xs_hi, 1)

            def x0t_out(c, par, use, first=False):
                act.wait_ge(misc_full, use + 1)
                if not first:
                    act.wait_ge(acc_step, c * (TILES * DVE_FIELDS) + (1 - TILES) * DVE_FIELDS)
                nc.scalar.activation(x0t[:, par, :, :].rearrange("p q f -> p (q f)"), misc[:, 0:TILES * (F + 1)],
                                     ACT.Copy).then_inc(x0t_ready, 1)
                act.wait_ge(x0t_ready, c + 1)
                act.sem_inc(misc_free, 1)

            def rep_out(c):
                act.wait_ge(rep_full, c + 1)
                act.wait_ge(z_ready, c * NT)
                nc.scalar.activation(rep, roll[0][0:PR, :], ACT.Copy).then_inc(rep_ready, 1)

            def x1_hi_out(c, par):
                act.wait_ge(l0_done, c * NT + NT)
                nc.scalar.activation(x1h[:, par, :], c0[:], ACT.Copy).then_inc(x1_hi, 1)

            def z_out(col, use, cnt):
                act.wait_ge(misc_full, use + 1)
                nc.scalar.activation(z_all[:, :, bass.ds(col, TB)].rearrange("p f b -> p b f"),
                                     misc[:, 0:ZF].rearrange("p (b f) -> p b f", f=F), ACT.Copy).then_inc(z_in, 1)
                nc.scalar.activation(out1[:, bass.ds(col, TB)], misc[:, ZF:ZC], ACT.Copy).then_inc(z_in, 1)
                act.wait_ge(z_in, cnt)
                act.sem_inc(misc_free, 1)

            def products(tau, k, q, j):
                g = ACT_GROUPS[j]
                n = tau * NA + j
                bank = ya[(q * NA + j) % 2]
                act.wait_ge(ya_full, n + 1)
                act.wait_ge(fold_step, tau * FOLDS + max(j, 1))
                for i, f in enumerate(fields(g)):
                    last = nc.scalar.activation(prod[:, j, i, :], bank[:, i * M:(i + 1) * M], ACT.Copy,
                                                scale=x0t[:, k % 2, q, f:f + 1])
                last.then_inc(prod_ready, 1)

            for j in range(4):
                t_hi(j, j, j)
            x0t_out(0, 0, 4, first=True)
            rep_out(0)
            x1_hi_out(0, 0)

            def block_body(bt, last):
                for k in range(CHUNKS):
                    ahead = not (last and k == CHUNKS - 1)
                    c = bt * CHUNKS + k
                    par = (k + 1) % 2
                    for n in range(SLOTS):
                        q, g = divmod(n, NG)
                        tau = bt * 16 + (k * TILES + q)
                        if g == 1:
                            z_out(bt * P + (k * TILES + q) * TB, z_use(bt, k, q, last), tau * 2 + 2)
                        if ahead and k == CHUNKS - 1 and n - 1 in T_SLOT:
                            j = T_SLOT[n - 1]
                            t_hi(0, misc_use(bt, k, "t", j), j)
                        if ahead and n == X0T_SLOT + 1:
                            x0t_out(c + 1, par, misc_use(bt, k, "x0t"))
                        if ahead and n == REP_SLOT + 1:
                            rep_out(c + 1)
                        if ahead and n == X1_SLOT:
                            x1_hi_out(c + 1, par)
                        if g in ACT_GROUPS:
                            products(tau, k, q, ACT_GROUPS.index(g))

            with act.Fori(0, BLOCKS - 1) as bt:
                block_body(bt, False)
            block_body(BLOCKS - 1, True)
            for i in range(2):
                z_out(B + i * TB, FLUSH + i, 2 * (BLOCKS * 16 + 1 + i))
            act.wait_ge(late_in, 16 * 5)
            for i in range(H1 // P):
                act.wait_ge(h1_full, i + 1)
                nc.scalar.activation(h1[:, i, :], [ya[0], yd[0], ya[1], yd[1]][i][:], ACT.Relu, bias=b1c[:, i:i + 1])\
                    .then_inc(h1_ready, 1)
            for i in range(H2 // P):
                act.wait_ge(h2_full, i + 1)
                nc.scalar.activation(h2[:, i, :], roll[i][:], ACT.Relu, bias=b2c[:, i:i + 1]).then_inc(h2_ready, 1)

        @block.vector
        def _(dve):
            nc.vector.memset(cur1[:, 2:4, :], 0.0).then_inc(startup, 1)
            nc.vector.memset(acc[:, 1, :, :], 0.0).then_inc(startup, 1)
            nc.vector.memset(fold[:, 1, 0:2 * M], 0.0).then_inc(startup, 1)
            nc.vector.memset(bdiag[:, 2:4, :], 0.0).then_inc(startup, 1)
            dve.wait_ge(startup, 4)
            dve.sem_inc(cur1_ready, 1)
            dve.sem_inc(fold_step, FOLDS)
            dve.sem_inc(acc_step, DVE_FIELDS)
            dve.sem_inc(bdiag_ready, 2)
            dve.wait_ge(const_in, 16 * 6)
            for q in range(TILES):
                nc.vector.tensor_copy(bdiag[:, q, ZF:ZC], mask[:]).then_inc(startup, 1)
            nc.vector.tensor_tensor(w0s[:].rearrange("p t m -> p (t m)"), w0s[:].rearrange("p t m -> p (t m)"), w0braw,
                                    ALU.add).then_inc(w0_ready, 1)
            dve.wait_ge(w1h_ready, 1)
            nc.vector.tensor_tensor(w1l[:].rearrange("p f m -> p (f m)"), w1raw,
                                    w1h[:].rearrange("p f m -> p (f m)").bitcast(f32), ALU.subtract).then_inc(w1l_ready, 1)

            def t_lo(n, j):
                dve.wait_ge(xs_hi, n)
                nc.vector.tensor_tensor(xs[LO:KX, :, 4 * j:4 * j + 4], misc[0:F, :].rearrange("p (d b) -> p b d", d=4),
                                        xs[0:F, :, 4 * j:4 * j + 4].bitcast(f32), ALU.subtract).then_inc(xs_ready, 1)
                dve.wait_ge(xs_ready, n)
                dve.sem_inc(misc_free, 1)

            def pair_products(c, t):
                dve.wait_ge(rep_ready, c + 1)
                dve.wait_ge(roll_full, c * NT + t + 1)
                if t >= 3:
                    dve.wait_ge(l0_done, c * NT + t - 2)
                nc.vector.tensor_tensor(z[:, t % 3, :], roll[(t + 1) % 2][0:PR, :], rep, ALU.mult).then_inc(z_ready, 1)

            def x1_lo_out(c, par, sample):
                dve.wait_ge(x1_hi, c + 1)
                nc.vector.tensor_tensor(x1l[:, par, :], c0[:], x1h[:, par, :].bitcast(f32), ALU.subtract)
                nc.vector.tensor_reduce(out0[:, bass.ds(sample, CB)], c0[:].rearrange("p (b d) -> p b d", d=D),
                                        AX.X, ALU.add).then_inc(x1_ready, 1)

            def combine(tau, q):
                dve.wait_ge(fold_step, (tau + 2) * FOLDS)
                dve.wait_ge(acc_step, (tau + 2) * DVE_FIELDS)
                both = acc[:, q % 2, :, :]
                nc.vector.tensor_tensor(both.rearrange("p c m -> p (c m)"), both.rearrange("p c m -> p (c m)"),
                                        fold[:, q % 2, 0:2 * M], ALU.add).then_inc(half_step, 1)
                dve.wait_ge(half_step, tau + 2)
                nc.vector.tensor_tensor(cur1[:, q, :], both[:, 0, :], both[:, 1, :], ALU.add).then_inc(cur1_ready, 1)

            def make_bdiag(c, tau, k, q):
                dve.wait_ge(x0t_ready, c + 1)
                dve.wait_ge(misc_full, 0 + 1)
                xt = x0t[:, k % 2, q, 0:F].unsqueeze(1).broadcast_to([P, TB, F])
                mk = mask[:].unsqueeze(2).broadcast_to([P, TB, F])
                nc.vector.tensor_tensor(bdiag[:, q, 0:ZF].rearrange("p (b f) -> p b f", f=F), xt, mk, ALU.mult)\
                    .then_inc(bdiag_ready, 1)

            def accumulate(tau, k, q, j):
                g = DVE_GROUPS[j]
                n = tau * ND + j
                bank = yd[(q * ND + j) % 2]
                step = (tau + 1) * DVE_FIELDS + (fields(g)[0] - FG * (j + 1))
                dve.wait_ge(yd_full, n + 1)
                for i, f in enumerate(fields(g)):
                    s = x0t[:, k % 2, q, f:f + 1]
                    y = bank[:, i * M:(i + 1) * M]
                    a = acc[:, q % 2, i % 2, :]
                    if j == 0 and i < 2:
                        last = nc.vector.tensor_scalar(a, y, s, None, ALU.mult)
                    else:
                        dve.wait_ge(acc_step, step + i - 1)
                        last = nc.vector.scalar_tensor_tensor(out=a, in0=y, scalar=s, in1=a, op0=ALU.mult, op1=ALU.add)
                    last.then_inc(acc_step, 1)

            for j in range(4):
                t_lo(j + 1, j)
            for t in range(NT):
                pair_products(0, t)
            x1_lo_out(0, 0, 0)

            def block_body(bt, last):
                for k in range(CHUNKS):
                    ahead = not (last and k == CHUNKS - 1)
                    c = bt * CHUNKS + k
                    for n in range(SLOTS):
                        q, g = divmod(n, NG)
                        tau = bt * 16 + (k * TILES + q)
                        if g == 0:
                            dve.wait_ge(z_in, tau * 2)
                            make_bdiag(c, tau, k, q)
                        if g == 8:
                            combine(tau - 1, (q - 1) % TILES)
                        if ahead and k == CHUNKS - 1 and n - 1 in T_SLOT:
                            t_lo(bt * 4 + 4 + T_SLOT[n - 1] + 1, T_SLOT[n - 1])
                        if ahead and n - 2 in ROLL_SLOT:
                            pair_products(c + 1, ROLL_SLOT[n - 2])
                        if ahead and n == X1_SLOT + 1:
                            x1_lo_out(c + 1, (k + 1) % 2, bt * P + (k + 1) * CB)
                        if g in DVE_GROUPS:
                            accumulate(tau, k, q, DVE_GROUPS.index(g))

            with dve.Fori(0, BLOCKS - 1) as bt:
                block_body(bt, False)
            block_body(BLOCKS - 1, True)
            combine(BLOCKS * 16 - 1, 3)
            dve.wait_ge(o2_full, 1)
            nc.vector.tensor_copy(out2, c0[:]).then_inc(o2_ready, 1)
            dve.wait_ge(y_full, 1)
            nc.vector.tensor_copy(yrow[:], misc[0:1, :]).then_inc(y_ready, 1)

        @block.tensor
        def _(pe):
            mm = nc.tensor.matmul

            def transpose_embeddings(j, use):
                pe.wait_ge(misc_free, use + 1)
                pe.sem_inc(t_start, 1)
                for i in range(4):
                    d = 4 * j + i
                    last = nc.tensor.transpose(misc[0:F, i * P:(i + 1) * P], emb[:, :, d], ident[:])
                last.then_inc(misc_full, 1)

            def x0t_mm(bt1, k, use):
                pe.wait_ge(xs_ready, bt1 * 4 + 4)
                pe.wait_ge(misc_free, use + 1)
                xv = xs[0:KX, :, :].rearrange("p b d -> p (b d)")
                for q in range(TILES):
                    last = mm(misc[:, q * (F + 1):(q + 1) * (F + 1)], xv[:, k * CPOS + q * P:k * CPOS + (q + 1) * P],
                              selt[:], start=True, stop=True)
                last.then_inc(misc_full, 1)

            def select_mm(bank, s, k):
                xv = xs[0:KX, :, :].rearrange("p b d -> p (b d)")
                return mm(bank[0:PR, :], sel[:, s, :], xv[:, k * CPOS:(k + 1) * CPOS], start=True, stop=True)

            def rep_mm(c, k):
                pe.wait_ge(z_ready, c * NT)
                select_mm(roll[0], NT, k).then_inc(rep_full, 1)

            def roll_mm(c, t, k):
                if t == 1:
                    pe.wait_ge(rep_ready, c + 1)
                if t >= 2:
                    pe.wait_ge(z_ready, c * NT + t - 1)
                select_mm(roll[(t + 1) % 2], t, k).then_inc(roll_full, 1)

            def l0_mm(c, t):
                if t == 0:
                    pe.wait_ge(x1_ready, c)
                pe.wait_ge(z_ready, c * NT + t + 1)
                mm(c0[:], w0s[:, t, :], z[:, t % 3, :], start=(t == 0), stop=(t == NT - 1)).then_inc(l0_done, 1)

            def l1_mm(tau, k, q, g):
                f0, nf = fields(g)[0], len(fields(g))
                par = k % 2
                hi = x1h[:, par, q * P:(q + 1) * P]
                lo = x1l[:, par, q * P:(q + 1) * P]
                wh = w1h[:, f0:f0 + nf, :].rearrange("p f m -> p (f m)")
                wl = w1l[:, f0:f0 + nf, :].rearrange("p f m -> p (f m)")
                if g in ACT_GROUPS:
                    j = ACT_GROUPS.index(g)
                    bank, full, n = ya[(q * NA + j) % 2], ya_full, tau * NA + j
                    pe.wait_ge(prod_ready, n + 1)
                else:
                    j = DVE_GROUPS.index(g)
                    bank, full, n = yd[(q * ND + j) % 2], yd_full, tau * ND + j
                    done = sum(len(fields(x)) for x in DVE_GROUPS[:j - 1]) if j else -len(fields(DVE_GROUPS[-1]))
                    pe.wait_ge(acc_step, (tau + 1) * DVE_FIELDS + done)
                o = bank[:, 0:nf * M]
                mm(o, hi, wh, start=True, stop=False)
                mm(o, hi, wl, start=False, stop=False)
                mm(o, lo, wh, start=False, stop=True).then_inc(full, 1)

            def z_mm(slot, q, use):
                pe.wait_ge(misc_free, use + 1)
                pe.wait_ge(bdiag_ready, slot + 1)
                pe.wait_ge(cur1_ready, slot + 1)
                mm(misc[:, 0:ZC], cur1[:, q, :], bdiag[:, q, :], start=True, stop=True).then_inc(misc_full, 1)

            pe.wait_ge(const_in, 16 * 6)
            pe.wait_ge(pads_zero, 1)
            pe.wait_ge(emb_in, 16 * F)
            for j in range(4):
                transpose_embeddings(j, j)
            pe.sem_inc(emb_used, 1)
            pe.wait_ge(sel_ready, 2)
            x0t_mm(0, 0, 4)
            rep_mm(0, 0)
            pe.wait_ge(w0_ready, 1)
            roll_mm(0, 0, 0)
            roll_mm(0, 1, 0)
            for t in range(NT):
                l0_mm(0, t)
                if t + 2 < NT:
                    roll_mm(0, t + 2, 0)
            pe.wait_ge(w1h_ready, 1)
            pe.wait_ge(w1l_ready, 1)
            pe.wait_ge(startup, 8)

            def block_body(bt, last):
                for k in range(CHUNKS):
                    ahead = not (last and k == CHUNKS - 1)
                    c = bt * CHUNKS + k
                    nk = (k + 1) % CHUNKS
                    nbt = bt + 1 if k == CHUNKS - 1 else bt
                    pe.wait_ge(x1_ready, c + 1)
                    for n in range(SLOTS):
                        q, g = divmod(n, NG)
                        tau = bt * 16 + (k * TILES + q)
                        if g == 0:
                            z_mm(tau, (q - 2) % TILES, z_use(bt, k, q, last))
                        if ahead and k == CHUNKS - 1 and n in T_SLOT:
                            if T_SLOT[n] == 0:
                                pe.wait_ge(emb_in, bt * (16 * F) + 32 * F)
                            transpose_embeddings(T_SLOT[n], misc_use(bt, k, "t", T_SLOT[n]))
                        if ahead and n == X0T_SLOT:
                            x0t_mm(nbt, nk, misc_use(bt, k, "x0t"))
                            if k == CHUNKS - 1:
                                pe.sem_inc(emb_used, 1)
                        if ahead and n == REP_SLOT:
                            rep_mm(c + 1, nk)
                        if ahead and n in ROLL_SLOT:
                            roll_mm(c + 1, ROLL_SLOT[n], nk)
                        if ahead and n in L0_SLOT:
                            l0_mm(c + 1, L0_SLOT[n])
                        l1_mm(tau, k, q, g)

            with pe.Fori(0, BLOCKS - 1) as bt:
                block_body(bt, False)
            block_body(BLOCKS - 1, True)
            for i in range(2):
                z_mm(BLOCKS * 16 + i, 2 + i, FLUSH + i)

            pe.wait_ge(late_in, 16 * 5)
            pe.wait_ge(z_in, 2 * (BLOCKS * 16 + 2))
            for f in range(F):
                last = mm(c0[:], w2s[:, f, :], z_all[:, f, PAD:], start=(f == 0), stop=(f == F - 1))
            last.then_inc(o2_full, 1)
            pe.wait_ge(mlp_in, 16 * 3)
            pe.wait_ge(acc_step, (BLOCKS * 16 + 1) * DVE_FIELDS)
            pe.wait_ge(prod_ready, BLOCKS * 16 * NA + 2)
            banks = [ya[0], yd[0], ya[1], yd[1]]
            for i in range(H1 // P):
                cols = slice(i * P, (i + 1) * P)
                mm(banks[i][:], wt1_sb[:, 0, cols], out0[:], start=True, stop=False)
                mm(banks[i][:], wt1_sb[:, 1, cols], out1[:, PAD:], start=False, stop=False)
                mm(banks[i][:], wt1_sb[0:DC, 3, cols], ctx_sb[:], start=False, stop=False)
            pe.wait_ge(o2_ready, 1)
            for i in range(H1 // P):
                cols = slice(i * P, (i + 1) * P)
                mm(banks[i][:], wt1_sb[:, 2, cols], out2, start=False, stop=True).then_inc(h1_full, 1)
            for kk in range(H1 // P):
                pe.wait_ge(h1_ready, kk + 1)
                for i in range(H2 // P):
                    last = mm(roll[i][:], wt2_sb[:, kk, i * P:(i + 1) * P], h1[:, kk, :], start=(kk == 0),
                              stop=(kk == H1 // P - 1))
                    if kk == H1 // P - 1:
                        last.then_inc(h2_full, 1)
            for kk in range(H2 // P):
                pe.wait_ge(h2_ready, kk + 1)
                last = mm(misc[0:1, :], w3c[:, kk:kk + 1], h2[:, kk, :], start=(kk == 0), stop=(kk == H2 // P - 1))
            last.then_inc(y_full, 1)


def pair_rows():
    f = np.arange(F)
    return [(f * F + (f + s) % F, ((f + s) % F) * F + f) for s in range(NSHIFT)]


def selections():
    s = np.zeros((KX, NT + 1, PR), np.float32)
    for t in range(NT + 1):
        for j in range(SH):
            shift = 0 if t == NT else SH * t + j
            if shift >= NSHIFT:
                continue
            for f in range(F):
                g = (f + shift) % F
                s[g, t, j * F + f] = s[LO + g, t, j * F + f] = 1.0
    return s


def kernel(**inputs):
    import concourse.bacc as _bacc
    from concourse.bass_utils import run_bass_kernel_spmd as _run

    a = {k: np.ascontiguousarray(v) for k, v in inputs.items()}
    w0 = a["L0_rec_f0"]
    w0a = np.zeros((PR, NT, M), w0.dtype)
    w0b = np.zeros((PR, NT, M), w0.dtype)
    for s, (ra, rb) in enumerate(pair_rows()):
        t, j = divmod(s, SH)
        w0a[j * F:(j + 1) * F, t] = w0[ra]
        if s:
            w0b[j * F:(j + 1) * F, t] = w0[rb]
    selt = np.zeros((KX, F + 1), np.float32)
    selt[np.arange(F), np.arange(F)] = selt[LO + np.arange(F), np.arange(F)] = 1.0
    mask = (np.arange(P)[:, None] // D == np.arange(TB)[None, :]).astype(np.float32)
    arrays = {"ids": a["ids"]}
    for f in range(F):
        arrays[f"tbl_{f}"] = a[f"tbl_{f}"]
    arrays.update(
        w0a=w0a.reshape(PR, NT * M), w0b=w0b.reshape(PR, NT * M), w1=a["L0_rec_f1"], w2=a["L0_rec_f2"],
        wt1=a["W_top1"], bt1=np.ascontiguousarray(a["b_top1"].reshape(-1, P).T),
        wt2=a["W_top2"], bt2=np.ascontiguousarray(a["b_top2"].reshape(-1, P).T),
        wt3=np.ascontiguousarray(a["W_top3"].reshape(-1, P).T), ctx_t=np.ascontiguousarray(a["dense_ctx"].T),
        sel=selections().reshape(KX, (NT + 1) * PR), selt=selt, ident=np.eye(P, dtype=np.float32), mask=mask)

    nc = _bacc.Bacc("TRN2", target_bir_lowering=False, num_devices=1)
    d = {k: nc.dram_tensor(f"in_{k}", v.shape, mybir.dt.from_np(v.dtype), kind="ExternalInput").ap()
         for k, v in arrays.items()}
    out = nc.dram_tensor("out_y", (B, 1), mybir.dt.float32, kind="ExternalOutput").ap()
    program(nc, d["ids"], [d[f"tbl_{f}"] for f in range(F)], d["w0a"], d["w0b"], d["w1"], d["w2"], d["wt1"], d["bt1"],
            d["wt2"], d["bt2"], d["wt3"], d["ctx_t"], d["sel"], d["selt"], d["ident"], d["mask"], out)
    r = _run(nc, [{f"in_{k}": v for k, v in arrays.items()}], core_ids=[0])
    return r.results[0]["out_y"]
```

```python
import numpy as np
import concourse.bass as bass
from concourse import mybir
from contextlib import ExitStack

B, F, D, M = 512, 39, 16, 128
P = 128
BLOCKS = B // P
TB = P // D
CHUNKS = 4
TILES = 4
CPOS = TILES * P
CB = TILES * TB
LO = 64
KX = LO + F
SH = 3
NT = 7
NSHIFT = (F + 1) // 2
PR = SH * F
FG = 4
NG = 10
ZF = TB * F
ZC = ZF + TB
PAD = 2 * TB
H1, H2 = 512, 256
DC = 16


def fields(g):
    return range(FG * g, min(FG * (g + 1), F))


ACT_GROUPS = [0, 2, 4, 5, 7, 9]
DVE_GROUPS = [1, 3, 6, 8]
NA, ND = len(ACT_GROUPS), len(DVE_GROUPS)
DVE_FIELDS = sum(len(fields(g)) for g in DVE_GROUPS)
POOL_GROUPS = 4
FOLDS = POOL_GROUPS
SUMS = 5

SLOTS = TILES * NG
Z_G = 3
SUM_G = {1: 0, 3: 1, 4: 2, 6: 3, 8: 4, 9: 5}
T_SLOT = {(2, 30): 0, (2, 32): 1, (2, 36): 2, (2, 38): 3}
X0T_SLOT = 9
REP_SLOT = 10
ROLL_SLOT = {11 + 5 * t // 2: t for t in range(NT)}
L0_SLOT = {17 + 5 * t // 2: t for t in range(NT)}
X1_SLOT = 34
EARLY = 16


def slots_back(k, n, back):
    return divmod(k * SLOTS + n - back, SLOTS)


def program(nc, ids, tables, w0a, w0b, w1, w2, wt1, bt1, wt2, bt2, wt3, ctx_t, sel_d, selt_d, ident_d, mask_d, out):
    f32 = mybir.dt.float32
    f32r = mybir.dt.float32r
    i32 = mybir.dt.int32
    ALU = mybir.AluOpType
    ACT = mybir.ActivationFunctionType
    AX = mybir.AxisListType

    stack = ExitStack()
    with stack:
        def sb(name, shape, dt=f32):
            return stack.enter_context(nc.sbuf_tensor(name, shape, dt))

        def pb(name):
            return stack.enter_context(nc.psum_tensor(name, [P, 512], f32))

        def sem(name):
            return stack.enter_context(nc.semaphore(name))

        w1h = sb("w1h", [P, F, M], f32r)
        w1l = sb("w1l", [P, F, M], f32r)
        w2s = sb("w2s", [P, F, M])
        z_all = sb("z_all", [P, F, PAD + B])
        w1raw = z_all[:, :, :].rearrange("p f b -> p (f b)")[:, 0:F * M]
        w0braw = z_all[0:PR, :, :].rearrange("p f b -> p (f b)")[:, F * M:F * M + NT * M]
        selraw = z_all[0:KX, :, :].rearrange("p f b -> p (f b)")[:, 7000:7000 + (NT + 1) * PR]
        seltraw = z_all[0:KX, :, :].rearrange("p f b -> p (f b)")[:, 8000:8000 + F + 1]
        w0s = sb("w0s", [PR, NT, M])
        x1h = sb("x1h", [P, 2, CPOS], f32r)
        x1l = sb("x1l", [P, 2, CPOS], f32r)
        xs = sb("xs", [P, P, D], f32r)
        sel = sb("sel", [KX, NT + 1, PR], f32r)
        selt = sb("selt", [KX, F + 1], f32r)
        ident = sb("ident", [P, P])
        mask = sb("mask", [P, TB])
        bdiag = sb("bdiag", [P, TILES, ZC])
        x0t = sb("x0t", [P, 2, TILES, F + 1])
        cur1 = sb("cur1", [P, TILES, M])
        acc = sb("acc", [P, 2, 2, M])
        fold = sb("fold", [P, 2, FG * M])
        out0 = sb("out0", [P, B])
        out1 = sb("out1", [P, PAD + B])
        idx = sb("idx", [P, F], i32)
        b1c = sb("b1c", [P, H1 // P])
        b2c = sb("b2c", [P, H2 // P])
        w3c = sb("w3c", [P, H2 // P])
        ctx_sb = sb("ctx_sb", [DC, B])
        yrow = sb("yrow", [1, B])
        arena = sb("arena", [P, 5744])
        prod = arena[:, 0:3072].rearrange("p (s f m) -> p s f m", s=NA, f=FG)
        rep = arena[0:PR, 3072:3584]
        z = arena[0:PR, 3584:5120].rearrange("p (s n) -> p s n", s=3)
        emb = arena[:, 5120:5120 + F * D].rearrange("p (f d) -> p f d", d=D)
        wt1_sb = arena[:, 0:2048].rearrange("p (k n) -> p k n", k=4)
        wt2_sb = arena[:, 2048:3072].rearrange("p (k n) -> p k n", k=4)
        h1 = arena[:, 3072:5120].rearrange("p (k n) -> p k n", k=4)
        out2 = arena[:, 5120:5632]
        h2 = fold

        ya = [pb("ya0"), pb("ya1")]
        yd = [pb("yd0"), pb("yd1")]
        roll = [pb("roll0"), pb("roll1")]
        c0 = pb("c0")
        misc = pb("misc")
        first_banks = [ya[0], yd[0], ya[1], yd[1]]

        idx_in = sem("idx_in")
        const_in = sem("const_in")
        w1_in = sem("w1_in")
        late_in = sem("late_in")
        mlp_in = sem("mlp_in")
        emb_in = sem("emb_in")
        out_done = sem("out_done")
        pads_zero = sem("pads_zero")
        startup = sem("startup")
        sel_ready = sem("sel_ready")
        w0_ready = sem("w0_ready")
        w1h_ready = sem("w1h_ready")
        w1l_ready = sem("w1l_ready")
        emb_used = sem("emb_used")
        t_start = sem("t_start")
        gather_start = sem("gather_start")
        t_full = sem("t_full")
        misc_full = sem("misc_full")
        misc_free = sem("misc_free")
        xs_hi = sem("xs_hi")
        xs_ready = sem("xs_ready")
        x0t_ready = sem("x0t_ready")
        rep_full = sem("rep_full")
        rep_ready = sem("rep_ready")
        roll_full = sem("roll_full")
        z_ready = sem("z_ready")
        l0_done = sem("l0_done")
        x1_hi = sem("x1_hi")
        x1_ready = sem("x1_ready")
        ya_full = sem("ya_full")
        yd_full = sem("yd_full")
        prod_ready = sem("prod_ready")
        acc_step = sem("acc_step")
        fold_step = sem("fold_step")
        bdiag_ready = sem("bdiag_ready")
        sum_step = sem("sum_step")
        cur1_ready = sem("cur1_ready")
        z_in = sem("z_in")
        o2_full = sem("o2_full")
        o2_ready = sem("o2_ready")
        h1_full = sem("h1_full")
        h1_ready = sem("h1_ready")
        h2_full = sem("h2_full")
        h2_ready = sem("h2_ready")
        y_full = sem("y_full")
        y_ready = sem("y_ready")

        block = stack.enter_context(nc.Block())

        def uses(last):
            order = []
            for k in range(CHUNKS):
                for n in range(SLOTS):
                    if n % NG == Z_G:
                        order.append(("z", k, n // NG))
                    if n == X0T_SLOT and not (last and k == CHUNKS - 1):
                        order.append(("x0t", k))
            return {what: n for n, what in enumerate(order)}

        USES = {False: uses(False), True: uses(True)}

        def misc_use(bt, last, *what):
            return bt * len(USES[False]) + (1 + USES[last][what])

        FLUSH = misc_use(BLOCKS - 1, True, "z", CHUNKS - 1, TILES - 1) + 1

        @block.sync
        def _(sp):
            sp.dma_start(idx[:], ids[0:P, :]).then_inc(idx_in, 16)
            sp.dma_start(selraw, sel_d).then_inc(const_in, 16)
            sp.dma_start(seltraw, selt_d).then_inc(const_in, 16)
            sp.dma_start(ident[:], ident_d).then_inc(const_in, 16)
            sp.dma_start(mask[:], mask_d).then_inc(const_in, 16)
            sp.dma_start(w0s[:].rearrange("p t m -> p (t m)"), w0a).then_inc(const_in, 16)
            sp.dma_start(w0braw, w0b).then_inc(const_in, 16)
            sp.dma_start(w1raw.rearrange("p (f m) -> p f m", m=M), w1.rearrange("(f g) m -> g f m", g=M)).then_inc(w1_in, 16)
            sp.dma_start(w2s[:], w2.rearrange("(f g) m -> g f m", g=M)).then_inc(late_in, 16)
            sp.dma_start(b1c[:], bt1).then_inc(late_in, 16)
            sp.dma_start(b2c[:], bt2).then_inc(late_in, 16)
            sp.dma_start(w3c[:], wt3).then_inc(late_in, 16)
            sp.dma_start(ctx_sb[:], ctx_t).then_inc(late_in, 16)
            with sp.Fori(0, BLOCKS - 1) as bt:
                sp.wait_ge(emb_in, bt * (16 * F) + 16 * F)
                sp.dma_start(idx[:], ids[bass.ds(bt * P + P, P), :]).then_inc(idx_in, 16)
            sp.wait_ge(cur1_ready, BLOCKS * 16 + 2)
            sp.wait_ge(x1_ready, BLOCKS * CHUNKS)
            sp.dma_start(wt1_sb[:, 0:3, :], wt1[0:3 * P, :].rearrange("(k p) n -> p k n", p=P)).then_inc(mlp_in, 16)
            sp.dma_start(wt1_sb[0:DC, 3, :], wt1[3 * P:3 * P + DC, :]).then_inc(mlp_in, 16)
            sp.dma_start(wt2_sb, wt2.rearrange("(k p) n -> p k n", p=P)).then_inc(mlp_in, 16)
            sp.wait_ge(y_ready, 1)
            sp.dma_start(out.rearrange("b o -> o b"), yrow[:]).then_inc(out_done, 16)
            sp.wait_ge(out_done, 16)

        @block.gpsimd
        def _(pool):
            def gather(f):
                nc.gpsimd.indirect_dma_start(emb[:, f, :], None, tables[f],
                                             bass.IndirectOffsetOnAxis(ap=idx[:, f:f + 1], axis=0)).then_inc(emb_in, 16)

            nc.gpsimd.memset(xs[32:LO, :, :].bitcast(f32), 0.0).then_inc(pads_zero, 1)
            pool.wait_ge(idx_in, 16)
            for f in range(F):
                gather(f)
            pool.wait_ge(idx_in, 32)
            pool.wait_ge(emb_used, 1)
            for f in range(EARLY):
                gather(f)

            def tile_sum(tau, q, extra):
                s = q % 2
                total = fold[:, s, :]
                base = (tau + 1) * FOLDS

                def group(j):
                    return prod[:, j, :, :].rearrange("p f m -> p (f m)")
                extra()
                pool.wait_ge(prod_ready, tau * NA + 4)
                pool.wait_ge(cur1_ready, tau + 1)
                nc.gpsimd.tensor_tensor(total, group(0), group(1), ALU.add).then_inc(fold_step, 1)
                for j in range(2, POOL_GROUPS):
                    extra()
                    pool.wait_ge(prod_ready, tau * NA + j + 3)
                    pool.wait_ge(fold_step, base + j - 1)
                    nc.gpsimd.tensor_tensor(total, total, group(j), ALU.add).then_inc(fold_step, 1)
                extra()
                pool.wait_ge(fold_step, base + POOL_GROUPS - 1)
                nc.gpsimd.tensor_tensor(fold[:, s, 0:2 * M], fold[:, s, 0:2 * M], fold[:, s, 2 * M:4 * M],
                                        ALU.add).then_inc(fold_step, 1)

            def block_body(bt, following):
                rest = list(range(EARLY, F)) if following > 0 else []
                early = list(range(EARLY)) if following > 1 else []
                for t in range(CHUNKS * TILES):
                    if t == 12 and early:
                        pool.wait_ge(idx_in, bt * 16 + 48)
                        pool.wait_ge(emb_used, bt + 2)
                        pool.sem_inc(gather_start, 1)
                        rest = early

                    def extra():
                        if rest:
                            gather(rest.pop(0))
                    tile_sum(bt * 16 + t, t % TILES, extra)

            with pool.Fori(0, BLOCKS - 2) as bt:
                block_body(bt, 2)
            block_body(BLOCKS - 2, 1)
            block_body(BLOCKS - 1, 0)

        @block.scalar
        def _(act):
            act.sem_inc(misc_free, 1)
            act.sem_inc(prod_ready, 2)
            act.wait_ge(const_in, 16 * 6)
            nc.scalar.activation(sel[:].rearrange("p t r -> p (t r)"), selraw, ACT.Copy).then_inc(sel_ready, 1)
            nc.scalar.activation(selt[:], seltraw, ACT.Copy).then_inc(sel_ready, 1)
            act.wait_ge(w1_in, 16)
            nc.scalar.activation(w1h[:].rearrange("p f m -> p (f m)"), w1raw, ACT.Copy).then_inc(w1h_ready, 1)

            def t_hi(n, j, bank):
                act.wait_ge(t_full, n)
                act.wait_ge(pads_zero, 1)
                nc.scalar.activation(xs[0:F, :, 4 * j:4 * j + 4], bank[0:F, :].rearrange("p (d b) -> p b d", d=4), ACT.Copy)\
                    .then_inc(xs_hi, 1)

            def x0t_out(c, par, use, first=False):
                act.wait_ge(misc_full, use + 1)
                if not first:
                    act.wait_ge(acc_step, c * (TILES * DVE_FIELDS) + (1 - TILES) * DVE_FIELDS)
                nc.scalar.activation(x0t[:, par, :, :].rearrange("p q f -> p (q f)"), misc[:, 0:TILES * (F + 1)],
                                     ACT.Copy).then_inc(x0t_ready, 1)
                act.wait_ge(x0t_ready, c + 1)
                act.sem_inc(misc_free, 1)

            def rep_out(c):
                act.wait_ge(rep_full, c + 1)
                act.wait_ge(z_ready, c * NT)
                nc.scalar.activation(rep, roll[0][0:PR, :], ACT.Copy).then_inc(rep_ready, 1)

            def x1_hi_out(c, par):
                act.wait_ge(l0_done, c * NT + NT)
                nc.scalar.activation(x1h[:, par, :], c0[:], ACT.Copy).then_inc(x1_hi, 1)

            def z_out(col, use, cnt):
                act.wait_ge(misc_full, use + 1)
                nc.scalar.activation(z_all[:, :, bass.ds(col, TB)].rearrange("p f b -> p b f"),
                                     misc[:, 0:ZF].rearrange("p (b f) -> p b f", f=F), ACT.Copy).then_inc(z_in, 1)
                nc.scalar.activation(out1[:, bass.ds(col, TB)], misc[:, ZF:ZC], ACT.Copy).then_inc(z_in, 1)
                act.wait_ge(z_in, cnt)
                act.sem_inc(misc_free, 1)

            def products(tau, k, q, j):
                g = ACT_GROUPS[j]
                n = tau * NA + j
                bank = ya[j % 2]
                act.wait_ge(ya_full, n + 1)
                if j < POOL_GROUPS:
                    act.wait_ge(fold_step, tau * FOLDS + max(j, 1))
                else:
                    act.wait_ge(sum_step, tau * SUMS + 2 * (j - POOL_GROUPS + 1))
                for i, f in enumerate(fields(g)):
                    last = nc.scalar.activation(prod[:, j, i, :], bank[:, i * M:(i + 1) * M], ACT.Copy,
                                                scale=x0t[:, k % 2, q, f:f + 1])
                last.then_inc(prod_ready, 1)

            for j in range(4):
                t_hi(j + 1, j, first_banks[j])
            x0t_out(0, 0, 0, first=True)
            rep_out(0)
            x1_hi_out(0, 0)

            def block_body(bt, last):
                for k in range(CHUNKS):
                    ahead = not (last and k == CHUNKS - 1)
                    c = bt * CHUNKS + k
                    par = (k + 1) % 2
                    for n in range(SLOTS):
                        q, g = divmod(n, NG)
                        tau = bt * 16 + (k * TILES + q)
                        if g == Z_G + 1:
                            z_out(bt * P + (k * TILES + q) * TB, misc_use(bt, last, "z", k, q), tau * 2 + 2)
                        if not last and slots_back(k, n, 1) in T_SLOT:
                            j = T_SLOT[slots_back(k, n, 1)]
                            t_hi(bt * 4 + 4 + j + 1, j, roll[j % 2])
                        if ahead and n == X0T_SLOT + 1:
                            x0t_out(c + 1, par, misc_use(bt, last, "x0t", k))
                        if ahead and n == REP_SLOT + 1:
                            rep_out(c + 1)
                        if ahead and n == X1_SLOT:
                            x1_hi_out(c + 1, par)
                        if g in ACT_GROUPS:
                            products(tau, k, q, ACT_GROUPS.index(g))

            with act.Fori(0, BLOCKS - 1) as bt:
                block_body(bt, False)
            block_body(BLOCKS - 1, True)
            for i in range(2):
                z_out(B + i * TB, FLUSH + i, 2 * (BLOCKS * 16 + 1 + i))
            act.wait_ge(late_in, 16 * 5)
            for i in range(H1 // P):
                act.wait_ge(h1_full, i + 1)
                nc.scalar.activation(h1[:, i, :], [ya[0], yd[0], ya[1], yd[1]][i][:], ACT.Relu, bias=b1c[:, i:i + 1])\
                    .then_inc(h1_ready, 1)
            for i in range(H2 // P):
                act.wait_ge(h2_full, i + 1)
                nc.scalar.activation(h2[:, i, :], roll[i][:], ACT.Relu, bias=b2c[:, i:i + 1]).then_inc(h2_ready, 1)

        @block.vector
        def _(dve):
            nc.vector.memset(cur1[:, 2:4, :], 0.0).then_inc(startup, 1)
            nc.vector.memset(acc[:, 1, :, :], 0.0).then_inc(startup, 1)
            nc.vector.memset(fold[:, 1, 0:2 * M], 0.0).then_inc(startup, 1)
            nc.vector.memset(bdiag[:, 2:4, :], 0.0).then_inc(startup, 1)
            nc.vector.memset(prod[:, 4:6, :, :], 0.0).then_inc(startup, 1)
            dve.wait_ge(startup, 5)
            dve.sem_inc(cur1_ready, 1)
            dve.sem_inc(fold_step, FOLDS)
            dve.sem_inc(acc_step, DVE_FIELDS)
            dve.sem_inc(bdiag_ready, 2)
            dve.wait_ge(const_in, 16 * 6)
            for q in range(TILES):
                nc.vector.tensor_copy(bdiag[:, q, ZF:ZC], mask[:]).then_inc(startup, 1)
            nc.vector.tensor_tensor(w0s[:].rearrange("p t m -> p (t m)"), w0s[:].rearrange("p t m -> p (t m)"), w0braw,
                                    ALU.add).then_inc(w0_ready, 1)
            dve.wait_ge(w1h_ready, 1)
            nc.vector.tensor_tensor(w1l[:].rearrange("p f m -> p (f m)"), w1raw,
                                    w1h[:].rearrange("p f m -> p (f m)").bitcast(f32), ALU.subtract).then_inc(w1l_ready, 1)

            def t_lo(n, j, bank):
                dve.wait_ge(xs_hi, n)
                nc.vector.tensor_tensor(xs[LO:KX, :, 4 * j:4 * j + 4], bank[0:F, :].rearrange("p (d b) -> p b d", d=4),
                                        xs[0:F, :, 4 * j:4 * j + 4].bitcast(f32), ALU.subtract).then_inc(xs_ready, 1)

            def pair_products(c, t):
                dve.wait_ge(rep_ready, c + 1)
                dve.wait_ge(roll_full, c * NT + t + 1)
                if t >= 3:
                    dve.wait_ge(l0_done, c * NT + t - 2)
                nc.vector.tensor_tensor(z[:, t % 3, :], roll[(t + 1) % 2][0:PR, :], rep, ALU.mult).then_inc(z_ready, 1)

            def x1_lo_out(c, par, sample):
                dve.wait_ge(x1_hi, c + 1)
                nc.vector.tensor_tensor(x1l[:, par, :], c0[:], x1h[:, par, :].bitcast(f32), ALU.subtract)
                nc.vector.tensor_reduce(out0[:, bass.ds(sample, CB)], c0[:].rearrange("p (b d) -> p b d", d=D),
                                        AX.X, ALU.add).then_inc(x1_ready, 1)

            def add_up(tau, q, step):
                both = acc[:, q % 2, :, :].rearrange("p c m -> p (c m)")
                g4 = prod[:, 4, :, :].rearrange("p f m -> p (f m)")
                g5 = prod[:, 5, :, :].rearrange("p f m -> p (f m)")
                if step == 0:
                    dve.wait_ge(acc_step, (tau + 2) * DVE_FIELDS)
                    dve.wait_ge(prod_ready, tau * NA + 7)
                elif step == 2:
                    dve.wait_ge(prod_ready, tau * NA + 8)
                elif step == 4:
                    dve.wait_ge(fold_step, (tau + 2) * FOLDS)
                if step > 0:
                    dve.wait_ge(sum_step, (tau + 1) * SUMS + step)
                if step == 3:
                    nc.vector.tensor_tensor(both[:, 0:M], both[:, 0:M], g5[:, 2 * M:3 * M], ALU.add).then_inc(sum_step, 1)
                elif step < SUMS:
                    part = (g4[:, 0:2 * M], g4[:, 2 * M:4 * M], g5[:, 0:2 * M], None, fold[:, q % 2, 0:2 * M])[step]
                    nc.vector.tensor_tensor(both, both, part, ALU.add).then_inc(sum_step, 1)
                else:
                    nc.vector.tensor_tensor(cur1[:, q, :], both[:, 0:M], both[:, M:2 * M], ALU.add).then_inc(cur1_ready, 1)

            def make_bdiag(c, tau, k, q):
                dve.wait_ge(x0t_ready, c + 1)
                xt = x0t[:, k % 2, q, 0:F].unsqueeze(1).broadcast_to([P, TB, F])
                mk = mask[:].unsqueeze(2).broadcast_to([P, TB, F])
                nc.vector.tensor_tensor(bdiag[:, q, 0:ZF].rearrange("p (b f) -> p b f", f=F), xt, mk, ALU.mult)\
                    .then_inc(bdiag_ready, 1)

            def accumulate(tau, k, q, j):
                g = DVE_GROUPS[j]
                n = tau * ND + j
                bank = yd[j % 2]
                step = (tau + 1) * DVE_FIELDS + sum(len(fields(x)) for x in DVE_GROUPS[:j])
                dve.wait_ge(yd_full, n + 1)
                if j == 0:
                    dve.wait_ge(cur1_ready, tau + 1)
                for i, f in enumerate(fields(g)):
                    s = x0t[:, k % 2, q, f:f + 1]
                    y = bank[:, i * M:(i + 1) * M]
                    a = acc[:, q % 2, i % 2, :]
                    if j == 0 and i < 2:
                        last = nc.vector.tensor_scalar(a, y, s, None, ALU.mult)
                    else:
                        dve.wait_ge(acc_step, step + i - 1)
                        last = nc.vector.scalar_tensor_tensor(out=a, in0=y, scalar=s, in1=a, op0=ALU.mult, op1=ALU.add)
                    last.then_inc(acc_step, 1)

            for j in range(4):
                t_lo(j + 1, j, first_banks[j])
            for t in range(NT):
                pair_products(0, t)
            x1_lo_out(0, 0, 0)

            def block_body(bt, last):
                for k in range(CHUNKS):
                    ahead = not (last and k == CHUNKS - 1)
                    c = bt * CHUNKS + k
                    for n in range(SLOTS):
                        q, g = divmod(n, NG)
                        tau = bt * 16 + (k * TILES + q)
                        if g == 0:
                            dve.wait_ge(z_in, tau * 2)
                            make_bdiag(c, tau, k, q)
                        if not last and slots_back(k, n, 2) in T_SLOT:
                            j = T_SLOT[slots_back(k, n, 2)]
                            t_lo(bt * 4 + 4 + j + 1, j, roll[j % 2])
                        if ahead and n - 1 in ROLL_SLOT:
                            pair_products(c + 1, ROLL_SLOT[n - 1])
                        if ahead and n == X1_SLOT + 1:
                            x1_lo_out(c + 1, (k + 1) % 2, bt * P + (k + 1) * CB)
                        if g in DVE_GROUPS:
                            accumulate(tau, k, q, DVE_GROUPS.index(g))
                        if g in SUM_G:
                            add_up(tau - 1, (q - 1) % TILES, SUM_G[g])

            with dve.Fori(0, BLOCKS - 1) as bt:
                block_body(bt, False)
            block_body(BLOCKS - 1, True)
            for step in range(SUMS + 1):
                add_up(BLOCKS * 16 - 1, 3, step)
            dve.wait_ge(o2_full, 1)
            nc.vector.tensor_copy(out2, c0[:]).then_inc(o2_ready, 1)
            dve.wait_ge(y_full, 1)
            nc.vector.tensor_copy(yrow[:], misc[0:1, :]).then_inc(y_ready, 1)

        @block.tensor
        def _(pe):
            mm = nc.tensor.matmul

            def transpose_embeddings(j, bank):
                for i in range(4):
                    d = 4 * j + i
                    last = nc.tensor.transpose(bank[0:F, i * P:(i + 1) * P], emb[:, :, d], ident[:])
                last.then_inc(t_full, 1)

            def x0t_mm(bt1, k, use):
                pe.wait_ge(xs_ready, bt1 * 4 + 4)
                pe.wait_ge(misc_free, use + 1)
                xv = xs[0:KX, :, :].rearrange("p b d -> p (b d)")
                for q in range(TILES):
                    last = mm(misc[:, q * (F + 1):(q + 1) * (F + 1)], xv[:, k * CPOS + q * P:k * CPOS + (q + 1) * P],
                              selt[:], start=True, stop=True)
                last.then_inc(misc_full, 1)

            def select_mm(bank, s, k):
                xv = xs[0:KX, :, :].rearrange("p b d -> p (b d)")
                return mm(bank[0:PR, :], sel[:, s, :], xv[:, k * CPOS:(k + 1) * CPOS], start=True, stop=True)

            def rep_mm(c, k):
                pe.wait_ge(z_ready, c * NT)
                select_mm(roll[0], NT, k).then_inc(rep_full, 1)

            def roll_mm(c, t, k):
                if t == 1:
                    pe.wait_ge(rep_ready, c + 1)
                if t >= 2:
                    pe.wait_ge(z_ready, c * NT + t - 1)
                select_mm(roll[(t + 1) % 2], t, k).then_inc(roll_full, 1)

            def l0_mm(c, t):
                if t == 0:
                    pe.wait_ge(x1_ready, c)
                pe.wait_ge(z_ready, c * NT + t + 1)
                mm(c0[:], w0s[:, t, :], z[:, t % 3, :], start=(t == 0), stop=(t == NT - 1)).then_inc(l0_done, 1)

            def l1_mm(tau, k, q, g):
                f0, nf = fields(g)[0], len(fields(g))
                par = k % 2
                hi = x1h[:, par, q * P:(q + 1) * P]
                lo = x1l[:, par, q * P:(q + 1) * P]
                wh = w1h[:, f0:f0 + nf, :].rearrange("p f m -> p (f m)")
                wl = w1l[:, f0:f0 + nf, :].rearrange("p f m -> p (f m)")
                if g in ACT_GROUPS:
                    j = ACT_GROUPS.index(g)
                    bank, full, n = ya[j % 2], ya_full, tau * NA + j
                    pe.wait_ge(prod_ready, n + 1)
                else:
                    j = DVE_GROUPS.index(g)
                    bank, full, n = yd[j % 2], yd_full, tau * ND + j
                    done = sum(len(fields(x)) for x in DVE_GROUPS[:j - 1]) if j else -len(fields(DVE_GROUPS[-1]))
                    pe.wait_ge(acc_step, (tau + 1) * DVE_FIELDS + done)
                o = bank[:, 0:nf * M]
                mm(o, hi, wh, start=True, stop=False)
                mm(o, hi, wl, start=False, stop=False)
                mm(o, lo, wh, start=False, stop=True).then_inc(full, 1)

            def z_mm(slot, q, use):
                pe.wait_ge(misc_free, use + 1)
                pe.wait_ge(bdiag_ready, slot + 1)
                pe.wait_ge(cur1_ready, slot + 1)
                mm(misc[:, 0:ZC], cur1[:, q, :], bdiag[:, q, :], start=True, stop=True).then_inc(misc_full, 1)

            pe.wait_ge(const_in, 16 * 6)
            pe.wait_ge(pads_zero, 1)
            pe.wait_ge(emb_in, 16 * F)
            for j in range(4):
                transpose_embeddings(j, first_banks[j])
            pe.wait_ge(t_full, 4)
            pe.sem_inc(emb_used, 1)
            pe.wait_ge(sel_ready, 2)
            x0t_mm(0, 0, 0)
            rep_mm(0, 0)
            pe.wait_ge(w0_ready, 1)
            roll_mm(0, 0, 0)
            roll_mm(0, 1, 0)
            for t in range(NT):
                l0_mm(0, t)
                if t + 2 < NT:
                    roll_mm(0, t + 2, 0)
            pe.wait_ge(w1h_ready, 1)
            pe.wait_ge(w1l_ready, 1)
            pe.wait_ge(startup, 9)

            def block_body(bt, last):
                for k in range(CHUNKS):
                    ahead = not (last and k == CHUNKS - 1)
                    c = bt * CHUNKS + k
                    nk = (k + 1) % CHUNKS
                    nbt = bt + 1 if k == CHUNKS - 1 else bt
                    pe.wait_ge(x1_ready, c + 1)
                    for n in range(SLOTS):
                        q, g = divmod(n, NG)
                        tau = bt * 16 + (k * TILES + q)
                        if g == Z_G:
                            z_mm(tau, (q - 2) % TILES, misc_use(bt, last, "z", k, q))
                        if not last and (k, n) in T_SLOT:
                            j = T_SLOT[k, n]
                            if j == 0:
                                pe.wait_ge(emb_in, bt * (16 * F) + 32 * F)
                                pe.wait_ge(z_ready, c * NT + 2 * NT)
                            elif j >= 2:
                                pe.wait_ge(xs_ready, bt * 4 + 4 + j - 1)
                            pe.sem_inc(t_start, 1)
                            transpose_embeddings(j, roll[j % 2])
                            if j == 3:
                                pe.wait_ge(t_full, bt * 4 + 8)
                                pe.sem_inc(emb_used, 1)
                        if ahead and n == X0T_SLOT:
                            x0t_mm(nbt, nk, misc_use(bt, last, "x0t", k))
                        if ahead and n == REP_SLOT:
                            rep_mm(c + 1, nk)
                        if ahead and n in ROLL_SLOT:
                            roll_mm(c + 1, ROLL_SLOT[n], nk)
                        if ahead and n in L0_SLOT:
                            l0_mm(c + 1, L0_SLOT[n])
                        l1_mm(tau, k, q, g)

            with pe.Fori(0, BLOCKS - 1) as bt:
                block_body(bt, False)
            block_body(BLOCKS - 1, True)
            for i in range(2):
                z_mm(BLOCKS * 16 + i, 2 + i, FLUSH + i)

            pe.wait_ge(late_in, 16 * 5)
            pe.wait_ge(z_in, 2 * (BLOCKS * 16 + 2))
            for f in range(F):
                last = mm(c0[:], w2s[:, f, :], z_all[:, f, PAD:], start=(f == 0), stop=(f == F - 1))
            last.then_inc(o2_full, 1)
            pe.wait_ge(mlp_in, 16 * 3)
            pe.wait_ge(acc_step, (BLOCKS * 16 + 1) * DVE_FIELDS)
            pe.wait_ge(prod_ready, BLOCKS * 16 * NA + 2)
            banks = [ya[0], yd[0], ya[1], yd[1]]
            for i in range(H1 // P):
                cols = slice(i * P, (i + 1) * P)
                mm(banks[i][:], wt1_sb[:, 0, cols], out0[:], start=True, stop=False)
                mm(banks[i][:], wt1_sb[:, 1, cols], out1[:, PAD:], start=False, stop=False)
                mm(banks[i][:], wt1_sb[0:DC, 3, cols], ctx_sb[:], start=False, stop=False)
            pe.wait_ge(o2_ready, 1)
            for i in range(H1 // P):
                cols = slice(i * P, (i + 1) * P)
                mm(banks[i][:], wt1_sb[:, 2, cols], out2, start=False, stop=True).then_inc(h1_full, 1)
            for kk in range(H1 // P):
                pe.wait_ge(h1_ready, kk + 1)
                for i in range(H2 // P):
                    last = mm(roll[i][:], wt2_sb[:, kk, i * P:(i + 1) * P], h1[:, kk, :], start=(kk == 0),
                              stop=(kk == H1 // P - 1))
                    if kk == H1 // P - 1:
                        last.then_inc(h2_full, 1)
            for kk in range(H2 // P):
                pe.wait_ge(h2_ready, kk + 1)
                last = mm(misc[0:1, :], w3c[:, kk:kk + 1], h2[:, kk, :], start=(kk == 0), stop=(kk == H2 // P - 1))
            last.then_inc(y_full, 1)


def pair_rows():
    f = np.arange(F)
    return [(f * F + (f + s) % F, ((f + s) % F) * F + f) for s in range(NSHIFT)]


def selections():
    s = np.zeros((KX, NT + 1, PR), np.float32)
    for t in range(NT + 1):
        for j in range(SH):
            shift = 0 if t == NT else SH * t + j
            if shift >= NSHIFT:
                continue
            for f in range(F):
                g = (f + shift) % F
                s[g, t, j * F + f] = s[LO + g, t, j * F + f] = 1.0
    return s


def kernel(**inputs):
    import concourse.bacc as _bacc
    from concourse.bass_utils import run_bass_kernel_spmd as _run

    a = {k: np.ascontiguousarray(v) for k, v in inputs.items()}
    w0 = a["L0_rec_f0"]
    w0a = np.zeros((PR, NT, M), w0.dtype)
    w0b = np.zeros((PR, NT, M), w0.dtype)
    for s, (ra, rb) in enumerate(pair_rows()):
        t, j = divmod(s, SH)
        w0a[j * F:(j + 1) * F, t] = w0[ra]
        if s:
            w0b[j * F:(j + 1) * F, t] = w0[rb]
    selt = np.zeros((KX, F + 1), np.float32)
    selt[np.arange(F), np.arange(F)] = selt[LO + np.arange(F), np.arange(F)] = 1.0
    mask = (np.arange(P)[:, None] // D == np.arange(TB)[None, :]).astype(np.float32)
    arrays = {"ids": a["ids"]}
    for f in range(F):
        arrays[f"tbl_{f}"] = a[f"tbl_{f}"]
    arrays.update(
        w0a=w0a.reshape(PR, NT * M), w0b=w0b.reshape(PR, NT * M), w1=a["L0_rec_f1"], w2=a["L0_rec_f2"],
        wt1=a["W_top1"], bt1=np.ascontiguousarray(a["b_top1"].reshape(-1, P).T),
        wt2=a["W_top2"], bt2=np.ascontiguousarray(a["b_top2"].reshape(-1, P).T),
        wt3=np.ascontiguousarray(a["W_top3"].reshape(-1, P).T), ctx_t=np.ascontiguousarray(a["dense_ctx"].T),
        sel=selections().reshape(KX, (NT + 1) * PR), selt=selt, ident=np.eye(P, dtype=np.float32), mask=mask)

    nc = _bacc.Bacc("TRN2", target_bir_lowering=False, num_devices=1)
    d = {k: nc.dram_tensor(f"in_{k}", v.shape, mybir.dt.from_np(v.dtype), kind="ExternalInput").ap()
         for k, v in arrays.items()}
    out = nc.dram_tensor("out_y", (B, 1), mybir.dt.float32, kind="ExternalOutput").ap()
    program(nc, d["ids"], [d[f"tbl_{f}"] for f in range(F)], d["w0a"], d["w0b"], d["w1"], d["w2"], d["wt1"], d["bt1"],
            d["wt2"], d["bt2"], d["wt3"], d["ctx_t"], d["sel"], d["selt"], d["ident"], d["mask"], out)
    r = _run(nc, [{f"in_{k}": v for k, v in arrays.items()}], core_ids=[0])
    return r.results[0]["out_y"]
```

```python
import numpy as np
import concourse.bass as bass
from concourse import mybir
from contextlib import ExitStack

B, F, D, M = 512, 39, 16, 128
P = 128
BLOCKS = B // P
TB = P // D
CHUNKS = 4
TILES = 4
CPOS = TILES * P
CB = TILES * TB
SH = 3
NT = 7
NSHIFT = (F + 1) // 2
FR = F + 1
PR = SH * FR
XR = SH * (NT - 1) + PR
NR = 4
STORES = -(-XR // F)
BPOS = P * D
FG = 4
NG = 10
ZF = TB * F
ZC = ZF + TB
PAD = 2 * TB
H1, H2 = 512, 256
L2_WHOLE = 4
L2_PARTS = [(4, 16), (16, 28), (28, 39)]
NZ = 3
DC = 16


def fields(g):
    return range(FG * g, min(FG * (g + 1), F))


ACT_GROUPS = [0, 2, 4, 5, 7, 9]
DVE_GROUPS = [1, 3, 6, 8]
NA, ND = len(ACT_GROUPS), len(DVE_GROUPS)
DVE_FIELDS = sum(len(fields(g)) for g in DVE_GROUPS)
POOL_GROUPS = 4
FOLDS = POOL_GROUPS
YA = 3
SUMS = 5

SLOTS = TILES * NG
Z_G = 4
ZOUT_G = 5
SUM_G = {1: 0, 3: 1, 4: 2, 6: 3, 8: 4, 9: 5}
T_SLOT = {(2, 30): 0, (2, 32): 1, (2, 35): 2, (2, 37): 3}
REPEAT_SLOT = (2, 26)
X0T_SLOT = 8
PROD_SLOT = {9 + 5 * t // 2: t for t in range(NT)}
L0_SLOT = {14 + 5 * t // 2: t for t in range(NT)}
X1_SLOT = 31
LAST_GATHERS = 6
WARM = (3, 6)
EARLY = 16


def slots_back(k, n, back):
    return divmod(k * SLOTS + n - back, SLOTS)


def program(nc, ids, tables, w0a, w0b, w1, w2, wt1, bt1, wt2, bt2, wt3, ctx_t, ident_d, mask_d, x0d, out):
    f32 = mybir.dt.float32
    f32r = mybir.dt.float32r
    i32 = mybir.dt.int32
    ALU = mybir.AluOpType
    ACT = mybir.ActivationFunctionType
    AX = mybir.AxisListType

    stack = ExitStack()
    with stack:
        def sb(name, shape, dt=f32):
            return stack.enter_context(nc.sbuf_tensor(name, shape, dt))

        def pb(name):
            return stack.enter_context(nc.psum_tensor(name, [P, 512], f32))

        def sem(name):
            return stack.enter_context(nc.semaphore(name))

        w1h = sb("w1h", [P, F, M], f32r)
        w1l = sb("w1l", [P, F, M], f32r)
        w2s = sb("w2s", [P, F, M])
        z_all = sb("z_all", [P, F, PAD + B])
        w1raw = z_all[:, :, :].rearrange("p f b -> p (f b)")[:, 0:F * M]
        w0braw = z_all[0:PR, :, :].rearrange("p f b -> p (f b)")[:, F * M:F * M + NT * M]
        w0s = sb("w0s", [PR, NT, M])
        x1h = sb("x1h", [P, 2, CPOS], f32r)
        x1l = sb("x1l", [P, 2, CPOS], f32r)
        xs = sb("xs", [PR, P, D])
        ident = sb("ident", [P, P])
        mask = sb("mask", [P, TB])
        bdiag = sb("bdiag", [P, TILES, ZC])
        x0t = sb("x0t", [P, 2, TILES, F + 1])
        cur1 = sb("cur1", [P, TILES, M])
        acc = sb("acc", [P, 2, 2, M])
        fold = sb("fold", [P, 2, FG * M])
        out0 = sb("out0", [P, B])
        out1 = sb("out1", [P, PAD + B])
        idx = sb("idx", [P, F], i32)
        b1c = sb("b1c", [P, H1 // P])
        b2c = sb("b2c", [P, H2 // P])
        w3c = sb("w3c", [P, H2 // P])
        arena = sb("arena", [P, 7040])
        prod = arena[:, 0:3072].rearrange("p (s f m) -> p s f m", s=NA, f=FG)
        z = arena[0:PR, 3072:5120].rearrange("p (s n) -> p s n", s=NR)
        emb3 = arena[:, 5120:5120 + PR * D].rearrange("p (j f d) -> p j f d", j=SH, d=D)
        emb = emb3[:, 0]
        wt1_sb = arena[:, 3072:5120].rearrange("p (k n) -> p k n", k=4)
        wt2_sb = arena[:, 2048:3072].rearrange("p (k n) -> p k n", k=4)
        h1 = arena[:, 0:2048].rearrange("p (k n) -> p k n", k=4)
        out2 = arena[:, 5120:5632]
        h2 = fold
        zh = [x1h[:, 0, :], x1h[:, 1, :], w1h[:, 0:B // M, :].rearrange("p f m -> p (f m)")]
        zl = [x1l[:, 0, :], x1l[:, 1, :], w1l[:, 0:B // M, :].rearrange("p f m -> p (f m)")]
        ctx_sb = xs[0:DC, 0:CB, :].rearrange("p b d -> p (b d)")
        yrow = acc[0:1].rearrange("p a s m -> p (a s m)")

        ya = [pb(f"ya{i}") for i in range(YA)]
        yd = [pb("yd0"), pb("yd1")]
        c0 = pb("c0")
        misc = [pb("misc0"), pb("misc1")]
        first_banks = [ya[0], yd[0], ya[1], yd[1]]
        mlp_banks = [*ya, c0]

        idx_in = sem("idx_in")
        const_in = sem("const_in")
        w1_in = sem("w1_in")
        late_in = sem("late_in")
        wt1_in = sem("wt1_in")
        wt2_in = sem("wt2_in")
        emb_in = sem("emb_in")
        out_done = sem("out_done")
        startup = sem("startup")
        w0_ready = sem("w0_ready")
        w1h_ready = sem("w1h_ready")
        w1l_ready = sem("w1l_ready")
        emb_repeated = sem("emb_repeated")
        emb_used = sem("emb_used")
        t_start = sem("t_start")
        gather_start = sem("gather_start")
        emb_last = sem("emb_last")
        first_full = sem("first_full")
        first_stored = sem("first_stored")
        first_in = [sem(f"first_in{t}") for t in range(NT)]
        misc_full = sem("misc_full")
        misc_free = sem("misc_free")
        xs_ready = sem("xs_ready")
        x0t_ready = sem("x0t_ready")
        x0d_done = sem("x0d_done")
        roll_in = [sem(f"roll_in{i}") for i in range(NR)]
        z_ready = sem("z_ready")
        l0_done = sem("l0_done")
        x1_hi = sem("x1_hi")
        x1_ready = sem("x1_ready")
        c0_read = sem("c0_read")
        ya_full = sem("ya_full")
        yd_full = sem("yd_full")
        prod_ready = sem("prod_ready")
        acc_step = sem("acc_step")
        fold_step = sem("fold_step")
        bdiag_ready = sem("bdiag_ready")
        sum_step = sem("sum_step")
        cur1_ready = sem("cur1_ready")
        z_in = sem("z_in")
        w2h_ready = sem("w2h_ready")
        w2l_pool = sem("w2l_pool")
        w2l_dve = sem("w2l_dve")
        zh_ready = sem("zh_ready")
        zl_ready = sem("zl_ready")
        l2_done = sem("l2_done")
        o2_ready = sem("o2_ready")
        h1_full = sem("h1_full")
        h1_ready = sem("h1_ready")
        h2_full = sem("h2_full")
        h2_ready = sem("h2_ready")
        y_full = sem("y_full")
        y_ready = sem("y_ready")

        block = stack.enter_context(nc.Block())

        def uses(last):
            order = []
            for k in range(CHUNKS):
                for n in range(SLOTS):
                    if n % NG == Z_G:
                        order.append(("z", k, n // NG))
                    if (k, n) in T_SLOT and not last:
                        order.append(("t", T_SLOT[k, n]))
                    if n == X0T_SLOT and not (last and k == CHUNKS - 1):
                        order.append(("x0t", k))
            return {what: n for n, what in enumerate(order)}

        USES = {False: uses(False), True: uses(True)}

        assert len(USES[False]) % 2 == 0

        def misc_use(bt, last, *what):
            n = 1 + USES[last][what]
            return bt * len(USES[False]) + n, misc[n % 2]

        LAST_USE = len(USES[False]) * (BLOCKS - 1) + 1 + len(USES[True])

        def rolled(k, t):
            return (k * NT + t) % NR

        def roll_loads(k, t):
            first_chunk = len(range(rolled(k, t), NT, NR))
            return (k * NT + t) // NR + 1 - first_chunk

        first_tiles = [z[:, t, :] if t < NR else arena[0:PR, (t - NR) * CPOS:(t - NR + 1) * CPOS] for t in range(NT)]

        def product_tile(k, t):
            return z[:, rolled(k, t), :]

        def transposed(bank):
            return bank[0:PR, :].rearrange("p (d b) -> p b d", d=4)

        def w2_part(w, part):
            lo, hi = L2_PARTS[part]
            return w[:, lo:hi, :].rearrange("p f m -> p (f m)")

        def w2_low(engine, part):
            return engine.tensor_tensor(w2_part(w1l, part), w2_part(w2s, part), w2_part(w1h, part).bitcast(f32), ALU.subtract)

        def store_first(queue, row):
            rows = min(F, XR - row)
            queue.dma_start(x0d[row:row + rows, 0:CPOS],
                            xs[0:rows, 0:CB, :].rearrange("p b d -> p (b d)")).then_inc(first_stored, 16)

        @block.sync
        def _(sp):
            sp.dma_start(idx[:], ids[0:P, :]).then_inc(idx_in, 16)
            sp.dma_start(ident[:], ident_d).then_inc(const_in, 16)
            sp.dma_start(mask[:], mask_d).then_inc(const_in, 16)
            sp.dma_start(w0s[:].rearrange("p t m -> p (t m)"), w0a).then_inc(const_in, 16)
            sp.dma_start(w0braw, w0b).then_inc(const_in, 16)
            sp.dma_start(w1raw.rearrange("p (f m) -> p f m", m=M), w1.rearrange("(f g) m -> g f m", g=M)).then_inc(w1_in, 16)
            sp.dma_start(w2s[:], w2.rearrange("(f g) m -> g f m", g=M)).then_inc(late_in, 16)
            sp.dma_start(b1c[:], bt1).then_inc(late_in, 16)
            sp.dma_start(b2c[:], bt2).then_inc(late_in, 16)
            sp.dma_start(w3c[:], wt3).then_inc(late_in, 16)

            def store_x0(bt, first=0):
                sp.wait_ge(xs_ready, bt * 4 + 4)
                for row in range(0, XR, F):
                    rows = min(F, XR - row)
                    sp.dma_start(x0d[row:row + rows, bass.ds(bt * BPOS + first * D, (P - first) * D)],
                                 xs[0:rows, first:P, :].rearrange("p b d -> p (b d)")).then_inc(x0d_done, 16)

            def load_rolled(bt, k, c):
                cols = bass.ds(bt * BPOS + k * CPOS, CPOS)
                for t in range(NT):
                    slot = rolled(k, t)
                    sp.wait_ge(l0_done, c * NT + t - NR + 1)
                    sp.dma_start(z[:, slot, :], x0d[SH * t:SH * t + PR, cols]).then_inc(roll_in[slot], 16)

            def next_indices(b):
                sp.wait_ge(emb_in, b * (16 * F) - 16 * LAST_GATHERS)
                sp.dma_start(idx[:], ids[bass.ds(b * P, P), :]).then_inc(idx_in, 16)

            sp.wait_ge(emb_last, 16 * LAST_GATHERS)
            next_indices(1)
            sp.wait_ge(xs_ready, 4)
            for row in range(0, 2 * F, F):
                store_first(sp, row)
            sp.wait_ge(first_stored, 16 * STORES)
            for t in range(NT):
                sp.dma_start(first_tiles[t], x0d[SH * t:SH * t + PR, 0:CPOS]).then_inc(first_in[t], 16)
            store_x0(0, CB)
            sp.wait_ge(x0d_done, 16 * STORES)

            def block_body(bt, following):
                for k in range(CHUNKS - 1):
                    load_rolled(bt, k + 1, bt * CHUNKS + (k + 1))
                if following > 1:
                    next_indices(bt + 2)
                if following > 0:
                    store_x0(bt + 1)
                    sp.wait_ge(x0d_done, (bt + 2) * (16 * STORES))
                    load_rolled(bt + 1, 0, bt * CHUNKS + CHUNKS)

            with sp.Fori(0, BLOCKS - 2) as bt:
                block_body(bt, 2)
            block_body(BLOCKS - 2, 1)
            block_body(BLOCKS - 1, 0)
            sp.wait_ge(x1_ready, BLOCKS * CHUNKS)
            sp.dma_start(ctx_sb, ctx_t).then_inc(wt1_in, 16)
            sp.dma_start(wt1_sb[:, 0:3, :], wt1[0:3 * P, :].rearrange("(k p) n -> p k n", p=P)).then_inc(wt1_in, 16)
            sp.dma_start(wt1_sb[0:DC, 3, :], wt1[3 * P:3 * P + DC, :]).then_inc(wt1_in, 16)
            sp.wait_ge(cur1_ready, BLOCKS * 16 + 2)
            sp.dma_start(wt2_sb, wt2.rearrange("(k p) n -> p k n", p=P)).then_inc(wt2_in, 16)
            sp.wait_ge(y_ready, 1)
            sp.dma_start(out.rearrange("b o -> o b"), yrow).then_inc(out_done, 16)
            sp.wait_ge(out_done, 16)

        @block.gpsimd
        def _(pool):
            def gather(f, done=emb_in):
                nc.gpsimd.indirect_dma_start(emb[:, f, :], None, tables[f],
                                             bass.IndirectOffsetOnAxis(ap=idx[:, f:f + 1], axis=0)).then_inc(done, 16)

            pool.wait_ge(idx_in, 16)
            for f in range(F):
                gather(f, emb_in if f < F - LAST_GATHERS else emb_last)
            pool.wait_ge(idx_in, 32)
            pool.wait_ge(emb_used, 1)
            for f in range(EARLY):
                gather(f)

            def tile_sum(tau, q, extra):
                s = q % 2
                total = fold[:, s, :]
                base = (tau + 1) * FOLDS

                def group(j):
                    return prod[:, j, :, :].rearrange("p f m -> p (f m)")
                extra()
                pool.wait_ge(prod_ready, tau * NA + (YA + 2))
                pool.wait_ge(cur1_ready, tau + 1)
                nc.gpsimd.tensor_tensor(total, group(0), group(1), ALU.add).then_inc(fold_step, 1)
                for j in range(2, POOL_GROUPS):
                    extra()
                    pool.wait_ge(prod_ready, tau * NA + (YA + j + 1))
                    pool.wait_ge(fold_step, base + j - 1)
                    nc.gpsimd.tensor_tensor(total, total, group(j), ALU.add).then_inc(fold_step, 1)
                extra()
                pool.wait_ge(fold_step, base + POOL_GROUPS - 1)
                nc.gpsimd.tensor_tensor(fold[:, s, 0:2 * M], fold[:, s, 0:2 * M], fold[:, s, 2 * M:4 * M],
                                        ALU.add).then_inc(fold_step, 1)

            def block_body(bt, following):
                rest = list(range(EARLY, F)) if following > 0 else []
                early = list(range(EARLY)) if following > 1 else []
                for t in range(CHUNKS * TILES):
                    if t == 12 and early:
                        pool.wait_ge(idx_in, bt * 16 + 48)
                        pool.wait_ge(emb_used, bt + 2)
                        pool.sem_inc(gather_start, 1)
                        rest = early

                    def extra():
                        if rest:
                            gather(rest.pop(0))
                    tile_sum(bt * 16 + t, t % TILES, extra)

            with pool.Fori(0, BLOCKS - 2) as bt:
                block_body(bt, 2)
            block_body(BLOCKS - 2, 1)
            block_body(BLOCKS - 1, 0)
            pool.wait_ge(late_in, 16 * 4)
            pool.wait_ge(w2h_ready, 1)
            w2_low(nc.gpsimd, 0).then_inc(w2l_pool, 1)

        @block.scalar
        def _(act):
            act.sem_inc(misc_free, 2)
            act.sem_inc(prod_ready, YA)
            act.wait_ge(w1_in, 16)
            nc.scalar.activation(w1h[:].rearrange("p f m -> p (f m)"), w1raw, ACT.Copy).then_inc(w1h_ready, 1)

            def repeat_embeddings(lo, hi):
                nc.scalar.activation(emb3[:, 1:SH, lo:hi, :], emb[:, lo:hi, :].unsqueeze(1).broadcast_to([P, SH - 1, hi - lo, D]),
                                     ACT.Copy).then_inc(emb_repeated, 1)

            def t_out(n, j, use):
                act.wait_ge(misc_full, use[0] + 1)
                if j == 0:
                    act.wait_ge(z_ready, (n - 1) * NT)
                nc.scalar.activation(xs[:, :, 4 * j:4 * j + 4], transposed(use[1]), ACT.Copy).then_inc(xs_ready, 1)
                act.wait_ge(xs_ready, n)
                act.sem_inc(misc_free, 1)

            def x0t_out(c, par, use, first=False):
                act.wait_ge(misc_full, use[0] + 1)
                if not first:
                    act.wait_ge(acc_step, c * (TILES * DVE_FIELDS) + (1 - TILES) * DVE_FIELDS)
                nc.scalar.activation(x0t[:, par, :, 0:F], use[1][:, 0:TILES * F].rearrange("p (q f) -> p q f", f=F),
                                     ACT.Copy).then_inc(x0t_ready, 1)
                act.wait_ge(x0t_ready, c + 1)
                act.sem_inc(misc_free, 1)

            def x1_hi_out(c, par):
                act.wait_ge(l0_done, c * NT + NT)
                nc.scalar.activation(x1h[:, par, :], c0[:], ACT.Copy).then_inc(x1_hi, 1)

            def z_out(col, use, cnt):
                act.wait_ge(misc_full, use[0] + 1)
                bank = use[1]
                nc.scalar.activation(z_all[:, :, bass.ds(col, TB)].rearrange("p f b -> p b f"),
                                     bank[:, 0:ZF].rearrange("p (b f) -> p b f", f=F), ACT.Copy).then_inc(z_in, 1)
                nc.scalar.activation(out1[:, bass.ds(col, TB)], bank[:, ZF:ZC], ACT.Copy).then_inc(z_in, 1)
                act.wait_ge(z_in, cnt)
                act.sem_inc(misc_free, 1)

            def products(tau, k, q, j):
                g = ACT_GROUPS[j]
                n = tau * NA + j
                bank = ya[j % YA]
                act.wait_ge(ya_full, n + 1)
                if j < POOL_GROUPS:
                    act.wait_ge(fold_step, tau * FOLDS + max(j, 1))
                else:
                    act.wait_ge(sum_step, tau * SUMS + 2 * (j - POOL_GROUPS + 1))
                for i, f in enumerate(fields(g)):
                    last = nc.scalar.activation(prod[:, j, i, :], bank[:, i * M:(i + 1) * M], ACT.Copy,
                                                scale=x0t[:, k % 2, q, f:f + 1])
                last.then_inc(prod_ready, 1)

            act.wait_ge(emb_in, 16 * (F - LAST_GATHERS))
            repeat_embeddings(0, F - LAST_GATHERS)
            act.wait_ge(startup, 6)
            act.wait_ge(emb_last, 16 * LAST_GATHERS)
            repeat_embeddings(F - LAST_GATHERS, FR)
            for j in range(0, 4, 2):
                act.wait_ge(first_full, j + 1)
                nc.scalar.activation(xs[:, :, 4 * j:4 * j + 4], transposed(first_banks[j]), ACT.Copy).then_inc(xs_ready, 1)
            act.wait_ge(xs_ready, 4)
            for row in range(2 * F, XR, F):
                store_first(act, row)
            x0t_out(0, 0, (0, misc[0]), first=True)
            x1_hi_out(0, 0)

            def block_body(bt, last):
                for k in range(CHUNKS):
                    ahead = not (last and k == CHUNKS - 1)
                    c = bt * CHUNKS + k
                    par = (k + 1) % 2
                    for n in range(SLOTS):
                        q, g = divmod(n, NG)
                        tau = bt * 16 + (k * TILES + q)
                        if g == ZOUT_G:
                            z_out(bt * P + (k * TILES + q) * TB, misc_use(bt, last, "z", k, q), tau * 2 + 2)
                        if not last and (k, n) == REPEAT_SLOT:
                            act.wait_ge(emb_in, bt * (16 * F) + 16 * (2 * F - LAST_GATHERS))
                            repeat_embeddings(0, FR)
                        if not last and slots_back(k, n, 1) in T_SLOT:
                            j = T_SLOT[slots_back(k, n, 1)]
                            t_out(bt * 4 + 4 + j + 1, j, misc_use(bt, last, "t", j))
                        if ahead and n == X0T_SLOT + 1:
                            x0t_out(c + 1, par, misc_use(bt, last, "x0t", k))
                        if ahead and n == X1_SLOT:
                            x1_hi_out(c + 1, par)
                        if g in ACT_GROUPS:
                            products(tau, k, q, ACT_GROUPS.index(g))

            with act.Fori(0, BLOCKS - 1) as bt:
                block_body(bt, False)
            block_body(BLOCKS - 1, True)
            def w2_high(part):
                nc.scalar.activation(w2_part(w1h, part), w2_part(w2s, part), ACT.Copy).then_inc(w2h_ready, 1)

            act.wait_ge(late_in, 16 * 4)
            w2_high(0)
            w2_high(1)
            for i in range(2):
                z_out(B + i * TB, (LAST_USE + i, misc[(LAST_USE + i) % 2]), 2 * (BLOCKS * 16 + 1 + i))
                if i == 0:
                    w2_high(2)
            for i in range(F - L2_WHOLE):
                if i >= NZ:
                    act.wait_ge(l2_done, i - NZ + 1)
                nc.scalar.activation(zh[i % NZ], z_all[:, L2_WHOLE + i, PAD:], ACT.Copy).then_inc(zh_ready, 1)
            for i in range(H1 // P):
                act.wait_ge(h1_full, i + 1)
                nc.scalar.activation(h1[:, i, :], mlp_banks[i][:], ACT.Relu, bias=b1c[:, i:i + 1])\
                    .then_inc(h1_ready, 1)
            for i in range(H2 // P):
                act.wait_ge(h2_full, i + 1)
                nc.scalar.activation(h2[:, i, :], yd[i][:], ACT.Relu, bias=b2c[:, i:i + 1]).then_inc(h2_ready, 1)

        @block.vector
        def _(dve):
            nc.vector.memset(cur1[:, 2:4, :], 0.0).then_inc(startup, 1)
            nc.vector.memset(acc[:, 1, :, :], 0.0).then_inc(startup, 1)
            nc.vector.memset(fold[:, 1, 0:2 * M], 0.0).then_inc(startup, 1)
            nc.vector.memset(bdiag[:, 2:4, :], 0.0).then_inc(startup, 1)
            nc.vector.memset(prod[:, 4:6, :, :], 0.0).then_inc(startup, 1)
            nc.vector.memset(emb[:, F, :], 0.0).then_inc(startup, 1)
            dve.wait_ge(startup, 6)
            dve.sem_inc(cur1_ready, 1)
            dve.sem_inc(fold_step, FOLDS)
            dve.sem_inc(acc_step, DVE_FIELDS)
            dve.sem_inc(bdiag_ready, 2)
            dve.wait_ge(const_in, 16 * 4)
            for q in range(TILES):
                nc.vector.tensor_copy(bdiag[:, q, ZF:ZC], mask[:]).then_inc(startup, 1)
            nc.vector.tensor_tensor(w0s[:].rearrange("p t m -> p (t m)"), w0s[:].rearrange("p t m -> p (t m)"), w0braw,
                                    ALU.add).then_inc(w0_ready, 1)
            dve.wait_ge(w1h_ready, 1)
            nc.vector.tensor_tensor(w1l[:].rearrange("p f m -> p (f m)"), w1raw,
                                    w1h[:].rearrange("p f m -> p (f m)").bitcast(f32), ALU.subtract).then_inc(w1l_ready, 1)

            def x0_of(k):
                return xs[:, k * CB:(k + 1) * CB, :].rearrange("p b d -> p (b d)")

            def pair_products(bt, k, c, t):
                dve.wait_ge(roll_in[rolled(k, t)], bt * (CHUNKS * NT // NR * 16) + 16 * roll_loads(k, t))
                nc.vector.tensor_tensor(product_tile(k, t), product_tile(k, t), x0_of(k), ALU.mult).then_inc(z_ready, 1)

            def x1_lo_out(c, par, sample):
                dve.wait_ge(x1_hi, c + 1)
                nc.vector.tensor_tensor(x1l[:, par, :], c0[:], x1h[:, par, :].bitcast(f32), ALU.subtract).then_inc(x1_ready, 1)
                nc.vector.tensor_reduce(out0[:, bass.ds(sample, CB)], c0[:].rearrange("p (b d) -> p b d", d=D),
                                        AX.X, ALU.add).then_inc(c0_read, 1)

            def add_up(tau, q, step):
                both = acc[:, q % 2, :, :].rearrange("p c m -> p (c m)")
                g4 = prod[:, 4, :, :].rearrange("p f m -> p (f m)")
                g5 = prod[:, 5, :, :].rearrange("p f m -> p (f m)")
                if step == 0:
                    dve.wait_ge(acc_step, (tau + 2) * DVE_FIELDS)
                    dve.wait_ge(prod_ready, tau * NA + (YA + 5))
                elif step == 2:
                    dve.wait_ge(prod_ready, tau * NA + (YA + 6))
                elif step == 4:
                    dve.wait_ge(fold_step, (tau + 2) * FOLDS)
                if step > 0:
                    dve.wait_ge(sum_step, (tau + 1) * SUMS + step)
                if step == 3:
                    nc.vector.tensor_tensor(both[:, 0:M], both[:, 0:M], g5[:, 2 * M:3 * M], ALU.add).then_inc(sum_step, 1)
                elif step < SUMS:
                    part = (g4[:, 0:2 * M], g4[:, 2 * M:4 * M], g5[:, 0:2 * M], None, fold[:, q % 2, 0:2 * M])[step]
                    nc.vector.tensor_tensor(both, both, part, ALU.add).then_inc(sum_step, 1)
                else:
                    nc.vector.tensor_tensor(cur1[:, q, :], both[:, 0:M], both[:, M:2 * M], ALU.add).then_inc(cur1_ready, 1)

            def make_bdiag(c, tau, k, q):
                dve.wait_ge(x0t_ready, c + 1)
                xt = x0t[:, k % 2, q, 0:F].unsqueeze(1).broadcast_to([P, TB, F])
                mk = mask[:].unsqueeze(2).broadcast_to([P, TB, F])
                nc.vector.tensor_tensor(bdiag[:, q, 0:ZF].rearrange("p (b f) -> p b f", f=F), xt, mk, ALU.mult)\
                    .then_inc(bdiag_ready, 1)

            def accumulate(tau, k, q, j):
                g = DVE_GROUPS[j]
                n = tau * ND + j
                bank = yd[j % 2]
                step = (tau + 1) * DVE_FIELDS + sum(len(fields(x)) for x in DVE_GROUPS[:j])
                dve.wait_ge(yd_full, n + 1)
                if j == 0:
                    dve.wait_ge(cur1_ready, tau + 1)
                for i, f in enumerate(fields(g)):
                    s = x0t[:, k % 2, q, f:f + 1]
                    y = bank[:, i * M:(i + 1) * M]
                    a = acc[:, q % 2, i % 2, :]
                    if j == 0 and i < 2:
                        last = nc.vector.tensor_scalar(a, y, s, None, ALU.mult)
                    else:
                        dve.wait_ge(acc_step, step + i - 1)
                        last = nc.vector.scalar_tensor_tensor(out=a, in0=y, scalar=s, in1=a, op0=ALU.mult, op1=ALU.add)
                    last.then_inc(acc_step, 1)

            for j in range(1, 4, 2):
                dve.wait_ge(first_full, j + 1)
                nc.vector.tensor_copy(xs[:, :, 4 * j:4 * j + 4], transposed(first_banks[j])).then_inc(xs_ready, 1)
            for t in range(NT):
                dve.wait_ge(first_in[t], 16)
                nc.vector.tensor_tensor(first_tiles[t], first_tiles[t], x0_of(0), ALU.mult).then_inc(z_ready, 1)
            x1_lo_out(0, 0, 0)

            def block_body(bt, last):
                for k in range(CHUNKS):
                    ahead = not (last and k == CHUNKS - 1)
                    c = bt * CHUNKS + k
                    nk = (k + 1) % CHUNKS
                    nbt = bt + 1 if k == CHUNKS - 1 else bt
                    for n in range(SLOTS):
                        q, g = divmod(n, NG)
                        tau = bt * 16 + (k * TILES + q)
                        if g == 0:
                            dve.wait_ge(z_in, tau * 2)
                            make_bdiag(c, tau, k, q)
                        if ahead and n in PROD_SLOT:
                            pair_products(nbt, nk, c + 1, PROD_SLOT[n])
                        if ahead and n == X1_SLOT + 1:
                            x1_lo_out(c + 1, (k + 1) % 2, bt * P + (k + 1) * CB)
                        if g in DVE_GROUPS:
                            accumulate(tau, k, q, DVE_GROUPS.index(g))
                        if g in SUM_G:
                            add_up(tau - 1, (q - 1) % TILES, SUM_G[g])

            with dve.Fori(0, BLOCKS - 1) as bt:
                block_body(bt, False)
            block_body(BLOCKS - 1, True)
            for step in range(SUMS + 1):
                add_up(BLOCKS * 16 - 1, 3, step)
            dve.wait_ge(late_in, 16 * 4)
            for part in (1, 2):
                dve.wait_ge(w2h_ready, part + 1)
                w2_low(nc.vector, part).then_inc(w2l_dve, 1)
            for i in range(F - L2_WHOLE):
                zf = z_all[:, L2_WHOLE + i, PAD:]
                dve.wait_ge(zh_ready, i + 1)
                nc.vector.tensor_tensor(zl[i % NZ], zf, zh[i % NZ].bitcast(f32), ALU.subtract).then_inc(zl_ready, 1)
            dve.wait_ge(l2_done, F - L2_WHOLE)
            nc.vector.tensor_copy(out2, misc[1][:]).then_inc(o2_ready, 1)
            dve.wait_ge(y_full, 1)
            nc.vector.tensor_copy(yrow, misc[0][0:1, :]).then_inc(y_ready, 1)

        @block.tensor
        def _(pe):
            mm = nc.tensor.matmul

            def transpose_embeddings(j, bank, full):
                for i in range(4):
                    d = 4 * j + i
                    last = nc.tensor.transpose(bank[0:PR, i * P:(i + 1) * P],
                                               emb3[:, :, :, d].rearrange("p j f -> p (j f)"), ident[:])
                last.then_inc(full, 1)

            def x0t_mm(bt1, k, use):
                pe.wait_ge(xs_ready, bt1 * 4 + 4)
                pe.wait_ge(misc_free, use[0] + 1)
                pe.sem_inc(t_start, 1)
                xv = xs[0:F].rearrange("p b d -> p (b d)")
                for q in range(TILES):
                    last = nc.tensor.transpose(use[1][:, q * F:(q + 1) * F], xv[:, k * CPOS + q * P:k * CPOS + (q + 1) * P],
                                               ident[0:F, 0:F])
                last.then_inc(misc_full, 1)

            def l0_mm(c, t, tile):
                if t == 0:
                    pe.wait_ge(c0_read, c)
                pe.wait_ge(z_ready, c * NT + t + 1)
                mm(c0[:], w0s[:, t, :], tile, start=(t == 0), stop=(t == NT - 1)).then_inc(l0_done, 1)

            def l1_mm(tau, k, q, g):
                f0, nf = fields(g)[0], len(fields(g))
                par = k % 2
                hi = x1h[:, par, q * P:(q + 1) * P]
                lo = x1l[:, par, q * P:(q + 1) * P]
                wh = w1h[:, f0:f0 + nf, :].rearrange("p f m -> p (f m)")
                wl = w1l[:, f0:f0 + nf, :].rearrange("p f m -> p (f m)")
                if g in ACT_GROUPS:
                    j = ACT_GROUPS.index(g)
                    bank, full, n = ya[j % YA], ya_full, tau * NA + j
                    pe.wait_ge(prod_ready, n + 1)
                else:
                    j = DVE_GROUPS.index(g)
                    bank, full, n = yd[j % 2], yd_full, tau * ND + j
                    done = sum(len(fields(x)) for x in DVE_GROUPS[:j - 1]) if j else -len(fields(DVE_GROUPS[-1]))
                    pe.wait_ge(acc_step, (tau + 1) * DVE_FIELDS + done)
                o = bank[:, 0:nf * M]
                mm(o, hi, wh, start=True, stop=False)
                mm(o, hi, wl, start=False, stop=False)
                mm(o, lo, wh, start=False, stop=True).then_inc(full, 1)

            def z_mm(slot, q, use):
                pe.wait_ge(misc_free, use[0] + 1)
                pe.wait_ge(bdiag_ready, slot + 1)
                pe.wait_ge(cur1_ready, slot + 1)
                mm(use[1][:, 0:ZC], cur1[:, q, :], bdiag[:, q, :], start=True, stop=True).then_inc(misc_full, 1)

            def warm_up(n):
                for _ in range(n):
                    mm(c0[:], ident[0:PR, :], w0s[:, 0:4, :].rearrange("p t m -> p (t m)"), start=True, stop=True)

            pe.wait_ge(const_in, 16 * 4)
            pe.wait_ge(w0_ready, 1)
            pe.wait_ge(emb_in, 16 * (F - LAST_GATHERS))
            warm_up(WARM[0])
            pe.wait_ge(emb_repeated, 2)
            for j in range(4):
                transpose_embeddings(j, first_banks[j], first_full)
            pe.wait_ge(first_full, 4)
            pe.sem_inc(emb_used, 1)
            x0t_mm(0, 0, (0, misc[0]))
            warm_up(WARM[1])
            for t in range(NT):
                l0_mm(0, t, first_tiles[t])
            pe.wait_ge(w1h_ready, 1)
            pe.wait_ge(w1l_ready, 1)
            pe.wait_ge(startup, 10)

            def block_body(bt, last):
                for k in range(CHUNKS):
                    ahead = not (last and k == CHUNKS - 1)
                    c = bt * CHUNKS + k
                    nk = (k + 1) % CHUNKS
                    nbt = bt + 1 if k == CHUNKS - 1 else bt
                    pe.wait_ge(x1_ready, c + 1)
                    for n in range(SLOTS):
                        q, g = divmod(n, NG)
                        tau = bt * 16 + (k * TILES + q)
                        if g == Z_G:
                            z_mm(tau, (q - 2) % TILES, misc_use(bt, last, "z", k, q))
                        if not last and (k, n) in T_SLOT:
                            j = T_SLOT[k, n]
                            use = misc_use(bt, last, "t", j)
                            if j == 0:
                                pe.wait_ge(emb_repeated, bt + 3)
                                pe.wait_ge(x0d_done, (bt + 1) * (16 * STORES))
                            pe.wait_ge(misc_free, use[0] + 1)
                            pe.sem_inc(t_start, 1)
                            transpose_embeddings(j, use[1], misc_full)
                            if j == 3:
                                pe.wait_ge(misc_full, use[0] + 1)
                                pe.sem_inc(emb_used, 1)
                        if ahead and n == X0T_SLOT:
                            x0t_mm(nbt, nk, misc_use(bt, last, "x0t", k))
                        if ahead and n in L0_SLOT:
                            l0_mm(c + 1, L0_SLOT[n], product_tile(nk, L0_SLOT[n]))
                        l1_mm(tau, k, q, g)

            with pe.Fori(0, BLOCKS - 1) as bt:
                block_body(bt, False)
            block_body(BLOCKS - 1, True)

            pe.wait_ge(late_in, 16 * 4)
            pe.wait_ge(wt1_in, 48)
            pe.wait_ge(prod_ready, BLOCKS * 16 * NA + YA)
            pe.wait_ge(c0_read, BLOCKS * CHUNKS)
            for i in range(H1 // P):
                cols = slice(i * P, (i + 1) * P)
                mm(mlp_banks[i][:], wt1_sb[:, 0, cols], out0[:], start=True, stop=False)
                mm(mlp_banks[i][:], wt1_sb[0:DC, 3, cols], ctx_sb, start=False, stop=False)
                if i < 2:
                    z_mm(BLOCKS * 16 + i, 2 + i, (LAST_USE + i, misc[(LAST_USE + i) % 2]))

            pe.wait_ge(z_in, 2 * (BLOCKS * 16 + 2))
            for f in range(L2_WHOLE):
                mm(misc[1][:], w2s[:, f, :], z_all[:, f, PAD:], start=(f == 0), stop=False)
            for i in range(F - L2_WHOLE):
                f = L2_WHOLE + i
                high = zh[i % NZ]
                if f == L2_PARTS[0][0]:
                    pe.wait_ge(w2l_pool, 1)
                elif f == L2_PARTS[1][0]:
                    pe.wait_ge(w2l_dve, 1)
                elif f == L2_PARTS[2][0]:
                    pe.wait_ge(w2l_dve, 2)
                pe.wait_ge(zh_ready, i + 1)
                mm(misc[1][:], w1h[:, f, :], high, start=False, stop=False)
                mm(misc[1][:], w1l[:, f, :], high, start=False, stop=False)
                pe.wait_ge(zl_ready, i + 1)
                mm(misc[1][:], w1h[:, f, :], zl[i % NZ], start=False, stop=(f == F - 1)).then_inc(l2_done, 1)
            for i in range(H1 // P):
                mm(mlp_banks[i][:], wt1_sb[:, 1, i * P:(i + 1) * P], out1[:, PAD:], start=False, stop=False)
            pe.wait_ge(o2_ready, 1)
            for i in range(H1 // P):
                mm(mlp_banks[i][:], wt1_sb[:, 2, i * P:(i + 1) * P], out2, start=False, stop=True).then_inc(h1_full, 1)
            pe.wait_ge(acc_step, (BLOCKS * 16 + 1) * DVE_FIELDS)
            pe.wait_ge(wt2_in, 16)
            for kk in range(H1 // P):
                pe.wait_ge(h1_ready, kk + 1)
                for i in range(H2 // P):
                    last = mm(yd[i][:], wt2_sb[:, kk, i * P:(i + 1) * P], h1[:, kk, :], start=(kk == 0),
                              stop=(kk == H1 // P - 1))
                    if kk == H1 // P - 1:
                        last.then_inc(h2_full, 1)
            for kk in range(H2 // P):
                pe.wait_ge(h2_ready, kk + 1)
                last = mm(misc[0][0:1, :], w3c[:, kk:kk + 1], h2[:, kk, :], start=(kk == 0), stop=(kk == H2 // P - 1))
            last.then_inc(y_full, 1)


def pair_rows():
    f = np.arange(F)
    return [(f * F + (f + s) % F, ((f + s) % F) * F + f) for s in range(NSHIFT)]


def kernel(**inputs):
    import concourse.bacc as _bacc
    from concourse.bass_utils import run_bass_kernel_spmd as _run

    a = {k: np.ascontiguousarray(v) for k, v in inputs.items()}
    w0 = a["L0_rec_f0"]
    w0a = np.zeros((PR, NT, M), w0.dtype)
    w0b = np.zeros((PR, NT, M), w0.dtype)
    for s, (ra, rb) in enumerate(pair_rows()):
        t, j = divmod(s, SH)
        w0a[j * FR:j * FR + F, t] = w0[ra]
        if s:
            w0b[j * FR:j * FR + F, t] = w0[rb]
    mask = (np.arange(P)[:, None] // D == np.arange(TB)[None, :]).astype(np.float32)
    arrays = {"ids": a["ids"]}
    for f in range(F):
        arrays[f"tbl_{f}"] = a[f"tbl_{f}"]
    arrays.update(
        w0a=w0a.reshape(PR, NT * M), w0b=w0b.reshape(PR, NT * M), w1=a["L0_rec_f1"], w2=a["L0_rec_f2"],
        wt1=a["W_top1"], bt1=np.ascontiguousarray(a["b_top1"].reshape(-1, P).T),
        wt2=a["W_top2"], bt2=np.ascontiguousarray(a["b_top2"].reshape(-1, P).T),
        wt3=np.ascontiguousarray(a["W_top3"].reshape(-1, P).T), ctx_t=np.ascontiguousarray(a["dense_ctx"].T),
        ident=np.eye(P, dtype=np.float32), mask=mask)

    nc = _bacc.Bacc("TRN2", target_bir_lowering=False, num_devices=1)
    d = {k: nc.dram_tensor(f"in_{k}", v.shape, mybir.dt.from_np(v.dtype), kind="ExternalInput").ap()
         for k, v in arrays.items()}
    out = nc.dram_tensor("out_y", (B, 1), mybir.dt.float32, kind="ExternalOutput").ap()
    x0d = nc.dram_tensor("x0_rolling", (XR, B * D), mybir.dt.float32, kind="Internal").ap()
    program(nc, d["ids"], [d[f"tbl_{f}"] for f in range(F)], d["w0a"], d["w0b"], d["w1"], d["w2"], d["wt1"], d["bt1"],
            d["wt2"], d["bt2"], d["wt3"], d["ctx_t"], d["ident"], d["mask"], x0d, out)
    r = _run(nc, [{f"in_{k}": v for k, v in arrays.items()}], core_ids=[0])
    return r.results[0]["out_y"]
```
